# Optimizing a Trainium2 kernel written in Bass

```python
import numpy as np
import jax
import jax.numpy as jnp

def _softmax(x, axis=-1):
    return jax.nn.softmax(x, axis=axis)

def _gelu(x):
    return jax.nn.gelu(x, approximate=True)

def _silu(x):
    return jax.nn.silu(x)

def _sigmoid(x):
    return jax.nn.sigmoid(x)

def _layernorm(x, axis=-1, eps=1e-05):
    m = jnp.mean(x, axis=axis, keepdims=True)
    v = jnp.var(x, axis=axis, keepdims=True)
    return (x - m) / jnp.sqrt(v + eps)

def _scatter_add(tgt, idx, src, axis=0):
    return tgt.at[idx].add(src)

def _segment_sum(src, seg, n):
    return jax.ops.segment_sum(src, seg, n)
kernel_name = 'mk_adaln_attn_ffn_d1_seqx_r8_d0218f'

def setup_inputs(seed: int=0):
    np.random.seed(seed)
    _w = jnp.asarray

    def _rec_inputs():
        import jax
        import jax.numpy as jnp
        _rk = jax.random.key(seed)
        x = -0.000125 + 0.9999 * jax.random.normal(jax.random.fold_in(_rk, 1), (32, 32, 512), jnp.float32)
        _lenS = 32 - jax.random.randint(jax.random.fold_in(_rk, 7), (32,), 0, max(1, 32 // 4) + 1, jnp.int32)
        _lenS2 = 32 - jax.random.randint(jax.random.fold_in(_rk, 8), (32,), 0, max(1, 32 // 4) + 1, jnp.int32)
        cond_128 = 0.0061147 + 1.02565 * jax.random.normal(jax.random.fold_in(_rk, 11), (32, 128), jnp.float32)
        fside_S_0 = -0.022604 + 0.987366 * jax.random.normal(jax.random.fold_in(_rk, 12), (32,), jnp.float32)
        return (x, cond_128, fside_S_0)
    x, cond_128, fside_S_0 = _rec_inputs()

    def _L0_cond_setup():
        import jax, jax.numpy as jnp
        import numpy as np
        K = 8
        T = 1.0
        D_EMBD = 128
        IN_C = 32
        OUT_C = 32
        BS = 32
        H = 512
        HID = 128
        key = jax.random.key(seed)
        ks = jax.random.split(key, 10)
        s = lambda fan_in: 1.0 / np.sqrt(fan_in)
        return {'x': jax.random.normal(ks[0], (BS, IN_C, H), dtype=jnp.float32), 'embedding': jax.random.normal(ks[1], (BS, D_EMBD), dtype=jnp.float32), 'W0': jax.random.normal(ks[2], (D_EMBD, HID), dtype=jnp.float32) * s(D_EMBD), 'b0': jnp.zeros((HID,), dtype=jnp.float32), 'W1': jax.random.normal(ks[3], (HID, HID), dtype=jnp.float32) * s(HID), 'b1': jnp.zeros((HID,), dtype=jnp.float32), 'W2': jax.random.normal(ks[4], (HID, K), dtype=jnp.float32) * s(HID), 'b2': jnp.zeros((K,), dtype=jnp.float32), 'weight': jax.random.normal(ks[5], (K, OUT_C, IN_C, 1), dtype=jnp.float32) * s(IN_C), 'bias_k': jax.random.normal(ks[6], (K, OUT_C), dtype=jnp.float32) * 0.1}
    _L0_cond_all = _L0_cond_setup()
    _L0_cond_in = {k: v for k, v in _L0_cond_all.items() if k in ('W0', 'b0', 'W1', 'b1', 'W2', 'b2', 'weight', 'bias_k')}
    del _L0_cond_all

    def _L0_attn_setup():
        import jax, jax.numpy as jnp
        import numpy as np
        HIDDEN = 512
        N_HEADS = 32
        N_KV_HEADS = 8
        HEAD_DIM = HIDDEN // N_HEADS
        N_REP = N_HEADS // N_KV_HEADS
        KV_DIM = N_KV_HEADS * HEAD_DIM

        def _kaiming_uniform(key, out_f, in_f):
            bound = 1.0 / np.sqrt(in_f)
            return jax.random.uniform(key, (out_f, in_f), jnp.float32, -bound, bound)

        def bitnet_linear(x, weight, scale_param):
            s = jnp.maximum(jnp.mean(jnp.abs(weight), axis=1), 1e-08)
            binary_w = jnp.sign(weight / s[:, None])
            y = jnp.einsum('bsi,oi->bso', x, binary_w)
            y = y * (s * scale_param)[None, None, :]
            return jnp.nan_to_num(y, nan=0.0, posinf=1000000.0, neginf=-1000000.0)
        key = jax.random.key(seed)
        ks = jax.random.split(key, 5)
        return {'hidden_states': jax.random.normal(ks[0], (1, 256, HIDDEN), jnp.float32), 'q_weight': _kaiming_uniform(ks[1], HIDDEN, HIDDEN), 'q_scale': jnp.ones((HIDDEN,), jnp.float32), 'k_weight': _kaiming_uniform(ks[2], KV_DIM, HIDDEN), 'k_scale': jnp.ones((KV_DIM,), jnp.float32), 'v_weight': _kaiming_uniform(ks[3], KV_DIM, HIDDEN), 'v_scale': jnp.ones((KV_DIM,), jnp.float32), 'o_weight': _kaiming_uniform(ks[4], HIDDEN, HIDDEN), 'o_scale': jnp.ones((HIDDEN,), jnp.float32)}
    _L0_attn_all = _L0_attn_setup()
    _L0_attn_in = {k: v for k, v in _L0_attn_all.items() if k in ('q_weight', 'q_scale', 'k_weight', 'k_scale', 'v_weight', 'v_scale', 'o_weight', 'o_scale')}
    del _L0_attn_all

    def _L0_cond2_setup():
        import jax, jax.numpy as jnp
        import numpy as np
        from jax import lax
        N, C_IN, L = (32, 32, 512)
        C_OUT, K, GROUPS = (32, 9, 4)
        C_DIM, PAD, STRIDE = (128, 4, 1)
        key = jax.random.key(seed)
        k1, k2, k3, k4, k5 = jax.random.split(key, 5)
        x = jax.random.normal(k1, (N, C_IN, L), dtype=jnp.float32)
        c = jax.random.normal(k2, (N, C_DIM), dtype=jnp.float32)
        weight = jax.random.normal(k3, (C_OUT, C_IN // GROUPS, K), dtype=jnp.float32)
        c_weight = jax.random.normal(k4, (C_OUT, C_DIM), dtype=jnp.float32)
        bias = jax.random.normal(k5, (C_OUT,), dtype=jnp.float32)
        return {'x': x, 'c': c, 'weight': weight, 'c_weight': c_weight, 'bias': bias}
    _L0_cond2_all = _L0_cond2_setup()
    _L0_cond2_in = {k: v for k, v in _L0_cond2_all.items() if k in ('weight', 'c_weight')}
    del _L0_cond2_all

    def _L0_ffn_setup():
        import jax, jax.numpy as jnp
        import numpy as np
        B_, S, D = (4, 512, 512)
        E, R, O = (8, 16, 512)
        TOP_K = 2
        SCALING = 8.0 / R
        key = jax.random.key(seed)
        ks = jax.random.split(key, 5)
        x = jax.random.normal(ks[0], (B_, S, D), dtype=jnp.float32)
        router_w = jax.random.normal(ks[1], (E, D), dtype=jnp.float32) * (1.0 / np.sqrt(D))
        router_b = jax.random.normal(ks[2], (E,), dtype=jnp.float32) * 0.01
        A = jax.random.normal(ks[3], (E, R, D), dtype=jnp.float32) * (1.0 / np.sqrt(D))
        Bm = jax.random.normal(ks[4], (E, O, R), dtype=jnp.float32) * 0.02
        return {'x': x, 'router_w': router_w, 'router_b': router_b, 'A': A, 'Bm': Bm}
    _L0_ffn_all = _L0_ffn_setup()
    _L0_ffn_in = {k: v for k, v in _L0_ffn_all.items() if k in ('router_w', 'router_b', 'A', 'Bm')}
    del _L0_ffn_all
    return {'x': x, 'cond_128': cond_128, 'fside_S_0': fside_S_0, 'L0_cond_W0': _L0_cond_in['W0'], 'L0_cond_b0': _L0_cond_in['b0'], 'L0_cond_W1': _L0_cond_in['W1'], 'L0_cond_b1': _L0_cond_in['b1'], 'L0_cond_W2': _L0_cond_in['W2'], 'L0_cond_b2': _L0_cond_in['b2'], 'L0_cond_weight': _L0_cond_in['weight'], 'L0_cond_bias_k': _L0_cond_in['bias_k'], 'L0_attn_q_weight': _L0_attn_in['q_weight'], 'L0_attn_q_scale': _L0_attn_in['q_scale'], 'L0_attn_k_weight': _L0_attn_in['k_weight'], 'L0_attn_k_scale': _L0_attn_in['k_scale'], 'L0_attn_v_weight': _L0_attn_in['v_weight'], 'L0_attn_v_scale': _L0_attn_in['v_scale'], 'L0_attn_o_weight': _L0_attn_in['o_weight'], 'L0_attn_o_scale': _L0_attn_in['o_scale'], 'L0_cond2_weight': _L0_cond2_in['weight'], 'L0_cond2_c_weight': _L0_cond2_in['c_weight'], 'L0_ffn_router_w': _L0_ffn_in['router_w'], 'L0_ffn_router_b': _L0_ffn_in['router_b'], 'L0_ffn_A': _L0_ffn_in['A'], 'L0_ffn_Bm': _L0_ffn_in['Bm']}

def reference(x, cond_128, fside_S_0, L0_cond_W0, L0_cond_b0, L0_cond_W1, L0_cond_b1, L0_cond_W2, L0_cond_b2, L0_cond_weight, L0_cond_bias_k, L0_attn_q_weight, L0_attn_q_scale, L0_attn_k_weight, L0_attn_k_scale, L0_attn_v_weight, L0_attn_v_scale, L0_attn_o_weight, L0_attn_o_scale, L0_cond2_weight, L0_cond2_c_weight, L0_ffn_router_w, L0_ffn_router_b, L0_ffn_A, L0_ffn_Bm):
    import jax
    import jax.numpy as jnp

    def _L0_cond_ref(x, embedding, W0, b0, W1, b1, W2, b2, weight, bias_k):
        import jax, jax.numpy as jnp
        import numpy as np
        K = 8
        T = 1.0
        D_EMBD = 128
        IN_C = 32
        OUT_C = 32
        BS = 32
        H = 512
        HID = 128
        h = jax.nn.gelu(embedding @ W0 + b0, approximate=False)
        h = jax.nn.gelu(h @ W1 + b1, approximate=False)
        att = jax.nn.softmax((h @ W2 + b2) / T, axis=-1)
        agg_w = jnp.einsum('bk,koi->boi', att, weight[..., 0])
        agg_b = att @ bias_k
        out = jnp.einsum('boi,bih->boh', agg_w, x) + agg_b[:, :, None]
        return out

    def _L0_attn_ref(hidden_states, q_weight, q_scale, k_weight, k_scale, v_weight, v_scale, o_weight, o_scale):
        import jax, jax.numpy as jnp
        import numpy as np
        HIDDEN = 512
        N_HEADS = 32
        N_KV_HEADS = 8
        HEAD_DIM = HIDDEN // N_HEADS
        N_REP = N_HEADS // N_KV_HEADS
        KV_DIM = N_KV_HEADS * HEAD_DIM

        def _kaiming_uniform(key, out_f, in_f):
            bound = 1.0 / np.sqrt(in_f)
            return jax.random.uniform(key, (out_f, in_f), jnp.float32, -bound, bound)

        def bitnet_linear(x, weight, scale_param):
            s = jnp.maximum(jnp.mean(jnp.abs(weight), axis=1), 1e-08)
            binary_w = jnp.sign(weight / s[:, None])
            y = jnp.einsum('bsi,oi->bso', x, binary_w)
            y = y * (s * scale_param)[None, None, :]
            return jnp.nan_to_num(y, nan=0.0, posinf=1000000.0, neginf=-1000000.0)
        b, s, _ = hidden_states.shape
        q = bitnet_linear(hidden_states, q_weight, q_scale)
        k = bitnet_linear(hidden_states, k_weight, k_scale)
        v = bitnet_linear(hidden_states, v_weight, v_scale)
        q = q.reshape(b, s, N_HEADS, HEAD_DIM).transpose(0, 2, 1, 3)
        k = k.reshape(b, s, N_KV_HEADS, HEAD_DIM).transpose(0, 2, 1, 3)
        v = v.reshape(b, s, N_KV_HEADS, HEAD_DIM).transpose(0, 2, 1, 3)
        k = jnp.repeat(k, N_REP, axis=1)
        v = jnp.repeat(v, N_REP, axis=1)
        scores = jnp.einsum('bhqd,bhkd->bhqk', q, k) / np.sqrt(HEAD_DIM)
        attn = jax.nn.softmax(scores, axis=-1)
        out = jnp.einsum('bhqk,bhkd->bhqd', attn, v)
        out = out.transpose(0, 2, 1, 3).reshape(b, s, HIDDEN)
        return bitnet_linear(out, o_weight, o_scale)

    def _L0_cond2_ref(x, c, weight, c_weight, bias):
        import jax, jax.numpy as jnp
        import numpy as np
        from jax import lax
        N, C_IN, L = (32, 32, 512)
        C_OUT, K, GROUPS = (32, 9, 4)
        C_DIM, PAD, STRIDE = (128, 4, 1)
        out = lax.conv_general_dilated(x, weight, window_strides=(STRIDE,), padding=[(PAD, PAD)], dimension_numbers=('NCH', 'OIH', 'NCH'), feature_group_count=GROUPS)
        ctx = jnp.einsum('nd,od->no', c, c_weight)
        out = out + ctx[:, :, None] + bias[None, :, None]
        return out

    def _L0_ffn_ref(x, router_w, router_b, A, Bm):
        import jax, jax.numpy as jnp
        import numpy as np
        B_, S, D = (4, 512, 512)
        E, R, O = (8, 16, 512)
        TOP_K = 2
        SCALING = 8.0 / R
        flat = x.reshape(-1, x.shape[-1])
        N = flat.shape[0]
        logits = flat @ router_w.T + router_b
        probs = jax.nn.softmax(logits, axis=-1)
        topv, topi = jax.lax.top_k(probs, TOP_K)
        gates = topv / jnp.sum(topv, axis=-1, keepdims=True)
        w = jnp.zeros((N, E), dtype=flat.dtype).at[jnp.arange(N)[:, None], topi].add(gates)
        h = jnp.einsum('nd,erd->ner', flat, A)
        hw = h * w[:, :, None]
        out = jnp.einsum('ner,eor->no', hw, Bm) * SCALING
        return out.reshape(*x.shape[:-1], O)
    x = x + _L0_attn_ref(_L0_cond_ref(x, cond_128, L0_cond_W0, L0_cond_b0, L0_cond_W1, L0_cond_b1, L0_cond_W2, L0_cond_b2, L0_cond_weight, L0_cond_bias_k), L0_attn_q_weight, L0_attn_q_scale, L0_attn_k_weight, L0_attn_k_scale, L0_attn_v_weight, L0_attn_v_scale, L0_attn_o_weight, L0_attn_o_scale)
    x = x + _L0_ffn_ref(_L0_cond2_ref(x, cond_128, L0_cond2_weight, L0_cond2_c_weight, fside_S_0), L0_ffn_router_w, L0_ffn_router_b, L0_ffn_A, L0_ffn_Bm)
    return x

_drawn_inputs = setup_inputs


def setup_inputs(seed=0):
    import zlib

    import numpy as np

    out = dict(_drawn_inputs(seed))
    spreads = {'L0_cond_b0': (0.0, 0.8),
     'L0_cond_b1': (0.0, 0.8),
     'L0_cond_b2': (0.0, 0.8),
     'L0_attn_q_scale': (1.0, 0.6),
     'L0_attn_k_scale': (1.0, 0.6),
     'L0_attn_v_scale': (1.0, 0.6),
     'L0_attn_o_scale': (1.0, 0.6)}
    factors = {'L0_cond_W0': 8.0,
     'L0_cond_W1': 4.73,
     'L0_cond_W2': 4.593,
     'L0_cond_weight': 2.892,
     'L0_cond_bias_k': 8.0,
     'L0_attn_q_weight': 8.0,
     'L0_attn_k_weight': 5.972,
     'L0_attn_v_weight': 3.152,
     'L0_attn_o_weight': 2.973,
     'L0_ffn_router_b': 200.0,
     'fside_S_0': 3.095}
    for name, (base, spread) in spreads.items():
        noise = np.random.default_rng([zlib.crc32(name.encode()), seed]).standard_normal(out[name].shape)
        drawn = base * np.exp(spread * noise) if base else spread * noise
        out[name] = jnp.asarray(drawn.astype(out[name].dtype))
    for name, factor in factors.items():
        out[name] = (out[name] * factor).astype(out[name].dtype)
    return out
```

```python
from contextlib import ExitStack

import concourse.bass as bass
from concourse import mybir

F32 = mybir.dt.float32
F32R = mybir.dt.float32r
I32 = mybir.dt.int32
U32 = mybir.dt.uint32
ALU = mybir.AluOpType
ACT = mybir.ActivationFunctionType
AX_X = mybir.AxisListType.X

P = 128
SAMPLES, TOKENS, HIDDEN = 32, 32, 512
PHASES = 4
STEPS = HIDDEN // PHASES
PER_TILE = P // TOKENS
TILES = SAMPLES // PER_TILE
ROWS = SAMPLES * TOKENS
MIXES = 8
GROUPS, MEMBERS, DIM = 8, 4, 16
BLOCKS = MEMBERS + 2
EXPERTS, RANK = 8, 16
FFN_COLS = EXPERTS * RANK + EXPERTS
PAIR = 2 * P
PAIRS = ROWS // PAIR
HALF = 2 * GROUPS
NAN_LIMIT = 1e6
FINITE_BOUND = 1e37

COND_COLS = dict(condT=SAMPLES, W0=P, b0=1, W1=P, b1=1, W2=MIXES, b2=MIXES, cwT=TOKENS)
MISC_COLS = dict(ident=P, headmask=GROUPS, iota=EXPERTS, router_b=EXPERTS, qkv_scale=BLOCKS, o_scale=PHASES)


def columns(widths):
    at, out = 0, {}
    for name, w in widths.items():
        out[name] = slice(at, at + w)
        at += w
    return out, at


COND, COND_W = columns(COND_COLS)
MISC, MISC_W = columns(MISC_COLS)


def build(nc, cond_pack, misc, mix_w, mix_b, x_rows, qkvT, qkv_rows, woT, wo_rows, conv_w, conv_b,
          ffn_in, ffn_out, out):
    with ExitStack() as ctx:
        def sb(name, shape, dt=F32):
            return ctx.enter_context(nc.sbuf_tensor(name, shape, dt))

        def sem(name):
            return ctx.enter_context(nc.semaphore(name))

        cond_sb = sb("cond_sb", [P, COND_W])
        misc_sb = sb("misc_sb", [P, MISC_W])
        mix_w_sb = sb("mix_w_sb", [P, TOKENS, MIXES])
        mix_b_sb = sb("mix_b_sb", [TILES * MIXES, TILES, TOKENS])
        x_all = sb("x_all", [P, TILES, HIDDEN])
        x_pair = sb("x_pair", [P, 2, HIDDEN])
        qkvT_sb = sb("qkvT_sb", [P, PHASES, BLOCKS * P])
        woT_sb = sb("woT_sb", [P, MEMBERS, HIDDEN])
        rows_sb = sb("rows_sb", [P, BLOCKS + PHASES, HIDDEN])
        conv_w_sb = sb("conv_w_sb", [P, 3, P])
        conv_b_sb = sb("conv_b_sb", [1, TOKENS])
        ffn_in_sb = sb("ffn_in_sb", [P, PHASES, FFN_COLS])
        ffn_out_sb = sb("ffn_out_sb", [P, HIDDEN])
        ones = sb("ones", [P, P])
        gelu0 = sb("gelu0", [P, SAMPLES])
        gelu1 = sb("gelu1", [P, SAMPLES])
        att = sb("att", [P, TILES, MIXES])
        att_red = sb("att_red", [P, 2, TILES])
        attT = sb("attT", [TILES * MIXES, P])
        agg = sb("agg", [P, TILES, TOKENS])
        agg_diag = sb("agg_diag", [P, TILES, PER_TILE, TOKENS])
        aggb_bc = sb("aggb_bc", [P, ROWS])
        convb_bc = sb("convb_bc", [P, ROWS])
        scale_in = sb("scale_in", [P, BLOCKS + PHASES])
        scale_all = sb("scale_all", [P, BLOCKS + PHASES])
        o_scale_bc = sb("o_scale_bc", [P, HIDDEN])
        qkv_sign = sb("qkv_sign", [P, PHASES, BLOCKS * P], F32R)
        wo_sign = sb("wo_sign", [P, MEMBERS, HIDDEN], F32R)
        sums = sb("sums", [P, 4])
        bound = sb("bound", [1, 8])
        safe_flag = sb("safe_flag", [1, 2], I32)
        mixed = sb("mixed", [P, PHASES, PAIR])
        gelu1_rep = mixed[:, :, :].rearrange("p a n -> p (a n)").rearrange("p (b o) -> p b o", o=TOKENS)
        mixed_hi = sb("mixed_hi", [P, PHASES, ROWS], F32R)
        mixed_lo = sb("mixed_lo", [P, PHASES, ROWS], F32R)
        qkv = sb("qkv", [P, BLOCKS, ROWS])
        junk = qkv[:, 0:MEMBERS, :].rearrange("p b n -> p (b n)")
        prod = qkv[:, MEMBERS:, :].rearrange("p b (t k) -> p (b t) k", k=MIXES).rearrange("p (t o) k -> p t o k", t=TILES)
        values_t = sb("values_t", [P, SAMPLES, 2 * DIM])
        q_tile = sb("q_tile", [P, PER_TILE, MEMBERS, TOKENS])
        keys_diag = sb("keys_diag", [P, PER_TILE, GROUPS, TOKENS])
        vals_diag = sb("vals_diag", [P, PER_TILE, 2, P])
        row_max = sb("row_max", [P, 2, HALF])
        probs = sb("probs", [P, 2, HALF, TOKENS])
        row_sum = sb("row_sum", [P, 2, HALF])
        row_inv = sb("row_inv", [P, 2, HALF])
        probs_n = sb("probs_n", [P, PER_TILE, GROUPS, TOKENS])
        outer_b = probs_n[0:TILES * MIXES, :, :, :].rearrange("p s g k -> p (s g) k").rearrange(
            "p (t q) o -> p t q o", q=PER_TILE)
        probsT = sb("probsT", [P, PER_TILE, 2, P])
        outer = probsT[:, :, :, :].rearrange("p s a n -> p (s a n)").rearrange("p (b o) -> p b o", o=TOKENS)
        attn_hi = sb("attn_hi", [P, MEMBERS, PER_TILE, TOKENS], F32R)
        attn_lo = sb("attn_lo", [P, MEMBERS, PER_TILE, TOKENS], F32R)
        o_out = sb("o_out", [P, HIDDEN])
        o_diag = o_out
        x1 = rows_sb[:, 0:TILES, :]
        x1_phased = sb("x1_phased", [P, PER_TILE, STEPS + 2])
        convT = sb("convT", [P, PHASES, PER_TILE, TOKENS])
        logits = sb("logits", [P, EXPERTS])
        logit_top = sb("logit_top", [P, 8])
        neg_max = sb("neg_max", [P, 1])
        gate_e = sb("gate_e", [P, EXPERTS])
        gate_top = sb("gate_top", [P, 8])
        gate_idx = sb("gate_idx", [P, 8], U32)
        gate_idx_f = sb("gate_idx_f", [P, 2])
        gate_sum = sb("gate_sum", [P, 1])
        gate_inv = sb("gate_inv", [P, 1])
        gate_two = sb("gate_two", [P, 2])
        gate_w = sb("gate_w", [P, 3, EXPERTS])
        gated = sb("gated", [P, P])
        gatedT = sb("gatedT", [P, P])
        g_low = rows_sb[:, TILES:, :].rearrange("p a n -> p (a n)")
        g_high = qkvT_sb[:, :, :].rearrange("p a n -> p (a n)")[:, 0:ROWS]
        g_fin = qkvT_sb[:, :, :].rearrange("p a n -> p (a n)")[:, ROWS:2 * ROWS].bitcast(I32)

        bank = [ctx.enter_context(nc.psum_tensor(f"bank{n}", [P, HIDDEN], F32)) for n in range(8)]
        ps_scores = bank[0:2]
        ps_probsT = bank[2:4]
        ps_attn, ps_y, ps_conv, ps_ffn = bank[4:8]
        attn_view = ps_attn[:, :].rearrange("p (s j q) -> p s j q", s=PER_TILE, j=MEMBERS)
        ps_mixed = bank[0:2]
        ps_qkv = bank[2:5]

        in_cond, in_misc, in_mix_w, in_mix_b = sem("in_cond"), sem("in_misc"), sem("in_mix_w"), sem("in_mix_b")
        in_pair, in_x = sem("in_pair"), sem("in_x")
        in_qkvT = [sem(f"in_qkvT{n}") for n in range(PHASES)]
        in_qkv_rows, in_wo_rows, in_woT = sem("in_qkv_rows"), sem("in_wo_rows"), sem("in_woT")
        in_conv_b, in_conv, in_ffn = sem("in_conv_b"), sem("in_conv"), sem("in_ffn")
        pool_const = sem("pool_const")
        pe_pro, dve_pro, act_pro = sem("pe_pro"), sem("dve_pro"), sem("act_pro")
        act_sign = sem("act_sign")
        act_sums = sem("act_sums")
        outer_done = sem("outer_done")
        agg_ready, aggb_ready, convb_ready = sem("agg_ready"), sem("aggb_ready"), sem("convb_ready")
        scale_ready, o_scale_ready = sem("scale_ready"), sem("o_scale_ready")
        mixed_done, mixed_full, hi_ready, lo_ready = sem("mixed_done"), sem("mixed_full"), sem("hi_ready"), sem("lo_ready")
        qkv_done, qkv_copied = sem("qkv_done"), sem("qkv_copied")
        qkv_guarded, values_turned = sem("qkv_guarded"), sem("values_turned")
        qkv_guard = [sem(f"qkv_guard{n}") for n in range(7)]
        o_guard = [sem(f"o_guard{n}") for n in range(7)]
        q_staged, keys_spread, values_spread = sem("q_staged"), sem("keys_spread"), sem("values_spread")
        scores_done, max_ready, shifted = sem("scores_done"), sem("max_ready"), sem("shifted")
        exp_ready, sum_ready, inv_ready = sem("exp_ready"), sem("sum_ready"), sem("inv_ready")
        probs_ready, probsT_done, probsT_copied = sem("probs_ready"), sem("probsT_done"), sem("probsT_copied")
        attn_done, attn_hi_ready, attn_lo_ready = sem("attn_done"), sem("attn_hi_ready"), sem("attn_lo_ready")
        y_done, y_scaled, x1_ready = sem("y_done"), sem("y_scaled"), sem("x1_ready")
        phased, conv_done, conv_biased = sem("phased"), sem("conv_done"), sem("conv_biased")
        ffn_in_done, gate_exp, gated_ready = sem("ffn_in_done"), sem("gate_exp"), sem("gated_ready")
        logits_ready, top_ready, neg_max_ready = sem("logits_ready"), sem("top_ready"), sem("neg_max_ready")
        gate_top_ready, gate_idx_ready, gate_sum_ready = sem("gate_top_ready"), sem("gate_idx_ready"), sem("gate_sum_ready")
        gate_inv_ready, gate_two_ready, idx_f_ready = sem("gate_inv_ready"), sem("gate_two_ready"), sem("idx_f_ready")
        share_ready, gate_w_ready = [sem("share_ready0"), sem("share_ready1")], sem("gate_w_ready")
        gatedT_done, gatedT_copied = sem("gatedT_done"), sem("gatedT_copied")
        ffn_done, out_ready, stored = sem("ffn_done"), sem("out_ready"), sem("stored")

        def reached(eng, s, n):
            if not isinstance(n, int) or n > 0:
                eng.wait_ge(s, n)

        ident = misc_sb[:, MISC["ident"]]

        def cols(i, width):
            return slice(i * width, (i + 1) * width) if isinstance(i, int) else bass.ds(i * width, width)

        def wait_apart(eng, s, n):
            if isinstance(n, int):
                eng.wait_ge(s, n)
            else:
                eng.wait_ge(s, 1)
                eng.wait_ge(s, n)

        PHASED_DMAS = PER_TILE * PHASES
        block = ctx.enter_context(nc.Block())

        @block.sync
        def _(sp):
            pair_rows = x_rows.rearrange("(i a p) n -> i p a n", p=P, a=2)
            sp.dma_start(cond_sb[:, :], cond_pack).then_inc(in_cond, 16)
            sp.dma_start(mix_w_sb[:, :, :], mix_w).then_inc(in_mix_w, 16)
            sp.dma_start(misc_sb[:, :], misc).then_inc(in_misc, 16)
            sp.dma_start(x_pair[:, :, :], pair_rows[0]).then_inc(in_pair, 16)
            sp.dma_start(mix_b_sb[:, :, :], mix_b).then_inc(in_mix_b, 16)
            sp.dma_start(conv_b_sb[:, :], conv_b).then_inc(in_conv_b, 16)
            for n in range(PHASES):
                sp.dma_start(qkvT_sb[:, n, :], qkvT[n]).then_inc(in_qkvT[n], 16)
            sp.dma_start(rows_sb[:, 0:BLOCKS, :], qkv_rows).then_inc(in_qkv_rows, 16)
            sp.dma_start(rows_sb[:, BLOCKS:, :], wo_rows).then_inc(in_wo_rows, 16)
            sp.dma_start(x_all[:, :, :], x_rows.rearrange("(t p) n -> p t n", p=P)).then_inc(in_x, 16)
            sp.wait_ge(mixed_done, 2)
            sp.dma_start(x_pair[:, :, :], pair_rows[1]).then_inc(in_pair, 16)
            sp.dma_start(woT_sb[:, :, :], woT).then_inc(in_woT, 16)
            sp.dma_start(conv_w_sb[:, :, :], conv_w).then_inc(in_conv, 16)
            sp.dma_start(ffn_in_sb[:, :, :], ffn_in).then_inc(in_ffn, 16)
            sp.dma_start(ffn_out_sb[:, :], ffn_out).then_inc(in_ffn, 16)
            for i in range(2, PAIRS):
                sp.wait_ge(mixed_done, 2 * i)
                sp.dma_start(x_pair[:, :, :], pair_rows[i]).then_inc(in_pair, 16)

            out_rows = out.rearrange("(t p) n -> t p n", p=P)

            def store(u):
                sp.wait_ge(out_ready, u + 1)
                if isinstance(u, int):
                    sp.dma_start(out_rows[u], x1[:, u, :]).then_inc(stored, 16)
                else:
                    sp.dma_start(out[bass.ds(u * P, P), :], x1[:, bass.ds(u, 1), :].rearrange("p a n -> p (a n)")
                                 ).then_inc(stored, 16)

            def to_phases(t):
                sp.wait_ge(x1_ready, t + 1)
                reached(sp, conv_done, t)
                for s in range(PER_TILE):
                    for ph in range(PHASES):
                        dst = x1_phased[TOKENS * ph:TOKENS * (ph + 1), s, 1:1 + STEPS]
                        if isinstance(t, int):
                            src = x1[TOKENS * s:TOKENS * (s + 1), t, STEPS * ph:STEPS * (ph + 1)]
                        else:
                            src = x1[TOKENS * s:TOKENS * (s + 1), bass.ds(t, 1), STEPS * ph:STEPS * (ph + 1)]
                            src = src.rearrange("p a n -> p (a n)")
                        sp.dma_start(dst, src).then_inc(phased, 16)

            to_phases(0)
            to_phases(1)
            with sp.Fori(2, TILES) as t:
                store(t - 2)
                to_phases(t)
            store(TILES - 2)
            store(TILES - 1)
            sp.wait_ge(stored, 16 * TILES)

        @block.gpsimd
        def _(pool):
            pool.memset(ones[:, :], 1.0).then_inc(pool_const, 1)
            pool.memset(agg_diag[:, :, :, :], 0.0).then_inc(pool_const, 1)
            pool.memset(vals_diag[:, :, :, :], 0.0).then_inc(pool_const, 1)
            pool.memset(x1_phased[:, :, :], 0.0).then_inc(pool_const, 1)
            pool.wait_ge(in_cond, 16)
            pool.tensor_tensor(outer[:, :, :],
                               cond_sb[:, COND["condT"]].unsqueeze(2).to_broadcast([P, SAMPLES, TOKENS]),
                               cond_sb[:, COND["cwT"]].unsqueeze(1).to_broadcast([P, SAMPLES, TOKENS]),
                               ALU.mult).then_inc(outer_done, 1)

            def stage_qk(t):
                if isinstance(t, int) and t == 0:
                    pool.wait_ge(qkv_guarded, 1)
                    pool.wait_ge(in_misc, 16)
                reached(pool, scores_done, 2 * t)
                pool.tensor_copy(q_tile[:, :, :, :].rearrange("p s j q -> p j s q"),
                                 qkv[:, 0:MEMBERS, cols(t, P)].rearrange("p j (s q) -> p j s q", q=TOKENS)
                                 ).then_inc(q_staged, 1)
                keys = qkv[:, MEMBERS, cols(t, P)].rearrange("p (s k) -> p s k", k=TOKENS)
                pool.tensor_tensor(keys_diag[:, :, :, :],
                                   keys.unsqueeze(2).to_broadcast([P, PER_TILE, GROUPS, TOKENS]),
                                   misc_sb[:, MISC["headmask"]].unsqueeze(1).unsqueeze(3)
                                   .to_broadcast([P, PER_TILE, GROUPS, TOKENS]),
                                   ALU.mult).then_inc(keys_spread, 1)

            def normalise(t):
                for h in range(2):
                    pool.wait_ge(inv_ready, 2 * t + h + 1)
                    reached(pool, probsT_done, 2 * t)
                    pool.tensor_tensor(probs_n[:, 2 * h:2 * h + 2, :, :].rearrange("p s g k -> p (s g) k"),
                                       probs[:, h, :, :],
                                       row_inv[:, h, :].unsqueeze(2).to_broadcast([P, HALF, TOKENS]),
                                       ALU.mult).then_inc(probs_ready, 1)

            def residual(t):
                pool.wait_ge(y_scaled, t + 1)
                if isinstance(t, int):
                    pool.tensor_tensor(x1[:, t, :], x_all[:, t, :], o_out[:, :], ALU.add).then_inc(x1_ready, 1)
                else:
                    pool.tensor_tensor(x1[:, bass.ds(t, 1), :].rearrange("p a n -> p (a n)"),
                                       x_all[:, bass.ds(t, 1), :].rearrange("p a n -> p (a n)"),
                                       o_out[:, :], ALU.add).then_inc(x1_ready, 1)

            stage_qk(0)
            pool.wait_ge(in_x, 16)
            stage_qk(1)
            normalise(0)
            with pool.Fori(0, TILES - 2) as t:
                stage_qk(t + 2)
                normalise(t + 1)
                residual(t)
            normalise(TILES - 1)
            residual(TILES - 2)
            residual(TILES - 1)

        @block.scalar
        def _(act):
            act.wait_ge(in_cond, 16)
            act.wait_ge(pe_pro, 1)
            nc.scalar.activation(gelu0[:, :], bank[0][:, 0:SAMPLES], ACT.Gelu,
                                 bias=cond_sb[:, COND["b0"]]).then_inc(act_pro, 1)
            act.wait_ge(pe_pro, 2)
            nc.scalar.activation(gelu1[:, :], bank[1][:, 0:SAMPLES], ACT.Gelu,
                                 bias=cond_sb[:, COND["b1"]]).then_inc(act_pro, 1)
            act.wait_ge(dve_pro, 4)
            nc.scalar.activation(att[:, :, :], att[:, :, :], ACT.Exp).then_inc(act_pro, 1)
            for n in range(PHASES):
                act.wait_ge(in_qkvT[n], 16)
                nc.scalar.activation(qkv_sign[:, n, :], qkvT_sb[:, n, :], ACT.Sign).then_inc(act_sign, 1)
            act.wait_ge(in_qkv_rows, 16)
            for n in range(BLOCKS + PHASES):
                if n == BLOCKS:
                    act.wait_ge(in_wo_rows, 16)
                nc.scalar.activation(junk[:, 0:HIDDEN], rows_sb[:, n, :], ACT.Abs,
                                     accum_out=scale_in[:, n:n + 1]).then_inc(act_sums, 1)
                act.wait_ge(act_sums, n + 1)
            act.wait_ge(in_x, 16)
            nc.scalar.activation(junk[:, :], x_all[:, :, :].rearrange("p t n -> p (t n)"), ACT.Abs,
                                 accum_out=sums[:, 0:1]).then_inc(act_sums, 1)

            def high_part(i):
                for b in range(2):
                    act.wait_ge(mixed_full, 2 * i + b + 1)
                    nc.scalar.activation(mixed_hi[:, 2 * b:2 * b + 2, cols(i, PAIR)],
                                         mixed[:, 2 * b:2 * b + 2, :], ACT.Copy).then_inc(hi_ready, 1)

            def scale_qkv(i):
                for b in range(3):
                    act.wait_ge(qkv_done, 3 * i + b + 1)
                    for n in (2 * b, 2 * b + 1):
                        nc.scalar.activation(qkv[:, n, cols(i, PAIR)],
                                             ps_qkv[b][:, (n % 2) * PAIR:(n % 2 + 1) * PAIR], ACT.Copy,
                                             scale=scale_all[:, n:n + 1]).then_inc(qkv_copied, 1)

            high_part(0)
            act.wait_ge(scale_ready, 1)
            with act.Fori(0, PAIRS - 1) as i:
                high_part(i + 1)
                scale_qkv(i)
            scale_qkv(PAIRS - 1)
            act.wait_ge(in_woT, 16)
            nc.scalar.activation(wo_sign[:, :, :], woT_sb[:, :, :], ACT.Sign).then_inc(act_sign, 1)

            def exponents(t):
                for h in range(2):
                    act.wait_ge(shifted, 2 * t + h + 1)
                    nc.scalar.activation(probs[:, h, :, :], probs[:, h, :, :], ACT.Exp,
                                         scale=float(DIM) ** -0.5).then_inc(exp_ready, 1)

            def copy_probsT(t):
                reached(act, attn_done, t)
                for h in range(2):
                    act.wait_ge(probsT_done, 2 * t + h + 1)
                    nc.scalar.activation(probsT[:, 2 * h:2 * h + 2, :, :].rearrange("p s a n -> p (s a n)"),
                                         ps_probsT[h][:, :], ACT.Copy).then_inc(probsT_copied, 1)

            def attn_high(t):
                act.wait_ge(attn_done, t + 1)
                reached(act, y_done, t)
                nc.scalar.activation(attn_hi[:, :, :, :].rearrange("p j s q -> p s j q"), attn_view, ACT.Copy).then_inc(attn_hi_ready, 1)

            def gate_exponents(u):
                act.wait_ge(neg_max_ready, u + 1)
                nc.scalar.activation(gate_e[:, :], logits[:, :], ACT.Exp, bias=neg_max[:, :]).then_inc(gate_exp, 1)

            def copy_gatedT(u):
                act.wait_ge(gatedT_done, u + 1)
                reached(act, ffn_done, u)
                nc.scalar.activation(gatedT[:, :], ps_ffn[:, PAIR:PAIR + P], ACT.Copy).then_inc(gatedT_copied, 1)

            def tile_step(t, scores=True, conv=True, ffn=True):
                copy_probsT(t)
                if scores:
                    exponents(t + 1)
                if ffn:
                    copy_gatedT(t - 2)
                attn_high(t)
                if conv:
                    gate_exponents(t - 1)

            exponents(0)
            tile_step(0, conv=False, ffn=False)
            tile_step(1, ffn=False)
            with act.Fori(2, TILES - 1) as t:
                tile_step(t)
            tile_step(TILES - 1, scores=False)
            copy_gatedT(TILES - 2)
            gate_exponents(TILES - 1)
            copy_gatedT(TILES - 1)

        @block.vector
        def _(dve):
            v = nc.vector
            count = [0]

            def done(ins):
                count[0] += 1
                ins.then_inc(dve_pro, 1)
                dve.wait_ge(dve_pro, count[0])

            dve.wait_ge(act_pro, 2)
            done(v.tensor_copy(gelu1_rep[:, :, :], gelu1[:, :].unsqueeze(2).to_broadcast([P, SAMPLES, TOKENS])))
            dve.wait_ge(pe_pro, 3)
            done(v.tensor_tensor(att[:, :, :], bank[2][:, 0:TILES * MIXES].rearrange("p (t k) -> p t k", k=MIXES),
                                 cond_sb[:, COND["b2"]].unsqueeze(1).to_broadcast([P, TILES, MIXES]), ALU.add))
            done(v.tensor_reduce(att_red[:, 0, :], att[:, :, :], AX_X, ALU.max))
            done(v.tensor_tensor(att[:, :, :], att[:, :, :],
                                 att_red[:, 0, :].unsqueeze(2).to_broadcast([P, TILES, MIXES]), ALU.subtract))
            dve.wait_ge(act_pro, 3)
            done(v.tensor_reduce(att_red[:, 0, :], att[:, :, :], AX_X, ALU.add))
            done(v.reciprocal(att_red[:, 1, :], att_red[:, 0, :]))
            done(v.tensor_tensor(att[:, :, :], att[:, :, :],
                                 att_red[:, 1, :].unsqueeze(2).to_broadcast([P, TILES, MIXES]), ALU.mult))
            dve.wait_ge(in_mix_w, 16)
            done(v.tensor_tensor(prod[:, :, :, :],
                                 att[:, :, :].unsqueeze(2).to_broadcast([P, TILES, TOKENS, MIXES]),
                                 mix_w_sb[:, :, :].unsqueeze(1).to_broadcast([P, TILES, TOKENS, MIXES]), ALU.mult))
            done(v.tensor_reduce(agg[:, :, :], prod[:, :, :, :], AX_X, ALU.add))
            dve.wait_ge(pool_const, 2)
            for q in range(PER_TILE):
                rows = slice(TOKENS * q, TOKENS * (q + 1))
                v.tensor_copy(agg_diag[rows, :, q, :], agg[rows, :, :]).then_inc(agg_ready, 1)
            dve.wait_ge(pe_pro, 4)
            done(v.tensor_copy(attT[:, :], bank[3][0:TILES * MIXES, 0:P]))
            dve.wait_ge(in_mix_b, 16)
            done(v.tensor_tensor(outer_b[:, :, :, :],
                                 attT[:, 0:P:TOKENS].unsqueeze(1).unsqueeze(3)
                                 .to_broadcast([TILES * MIXES, TILES, PER_TILE, TOKENS]),
                                 mix_b_sb[:, :, :].unsqueeze(2)
                                 .to_broadcast([TILES * MIXES, TILES, PER_TILE, TOKENS]), ALU.mult))
            dve.wait_ge(pe_pro, 5)
            for b in range(2):
                v.tensor_copy(aggb_bc[:, b * HIDDEN:(b + 1) * HIDDEN], bank[4 + b][:, :]).then_inc(aggb_ready, 1)

            def full_mixed(i):
                for b in range(2):
                    dve.wait_ge(mixed_done, 2 * i + b + 1)
                    reached(dve, lo_ready, 2 * i)
                    bias = aggb_bc[:, cols(i, PAIR)].unsqueeze(1).to_broadcast([P, 2, PAIR])
                    v.tensor_tensor(mixed[:, 2 * b:2 * b + 2, :],
                                    ps_mixed[b][:, :].rearrange("p (a n) -> p a n", a=2), bias,
                                    ALU.add).then_inc(mixed_full, 1)

            def low_part(i):
                for b in range(2):
                    dve.wait_ge(hi_ready, 2 * i + b + 1)
                    v.tensor_tensor(mixed_lo[:, 2 * b:2 * b + 2, cols(i, PAIR)], mixed[:, 2 * b:2 * b + 2, :],
                                    mixed_hi[:, 2 * b:2 * b + 2, cols(i, PAIR)].bitcast(F32),
                                    ALU.subtract).then_inc(lo_ready, 1)

            dve.wait_ge(aggb_ready, 2)
            full_mixed(0)
            low_part(0)

            dve.wait_ge(act_sums, BLOCKS + PHASES)
            dve.wait_ge(in_misc, 16)
            done(v.tensor_scalar(scale_in[:, :], scale_in[:, :], 1.0 / HIDDEN, 1e-8, ALU.mult, ALU.max))
            v.tensor_tensor(scale_all[:, 0:BLOCKS], scale_in[:, 0:BLOCKS], misc_sb[:, MISC["qkv_scale"]],
                            ALU.mult).then_inc(scale_ready, 1)
            v.tensor_tensor(scale_all[:, BLOCKS:], scale_in[:, BLOCKS:], misc_sb[:, MISC["o_scale"]],
                            ALU.mult).then_inc(scale_ready, 1)
            dve.wait_ge(scale_ready, 2)
            done(v.tensor_tensor(o_diag[:, :].rearrange("p (a n) -> p a n", a=PHASES),
                                 scale_all[:, BLOCKS:].unsqueeze(2).to_broadcast([P, PHASES, P]),
                                 ident.unsqueeze(1).to_broadcast([P, PHASES, P]), ALU.mult))
            for n, values in ((1, agg[:, :, :].rearrange("p t o -> p (t o)")), (2, aggb_bc[:, :]), (3, scale_all[:, :])):
                scratch = g_low[:, 0:values.shape[1]]
                done(v.scalar_tensor_tensor(out=scratch, in0=values, scalar=-1.0, in1=values, op0=ALU.mult,
                                            op1=ALU.max))
                done(v.tensor_reduce(sums[:, n:n + 1], scratch, AX_X, ALU.add))
            dve.wait_ge(pe_pro, 6)
            done(v.tensor_copy(bound[:, 0:4], bank[7][0:1, 0:4]))
            done(v.scalar_tensor_tensor(out=bound[:, 4:5], in0=bound[:, 0:1], scalar=bound[:, 1:2], in1=bound[:, 2:3],
                                        op0=ALU.mult, op1=ALU.add))
            done(v.tensor_scalar(bound[:, 5:6], bound[:, 4:5], bound[:, 3:4], float(HIDDEN), ALU.mult, ALU.mult))
            done(v.tensor_scalar(bound[:, 6:7], bound[:, 5:6], bound[:, 5:6], 4.0 * DIM, ALU.mult, ALU.mult))
            done(v.tensor_scalar(bound[:, 7:8], bound[:, 5:6], bound[:, 3:4], float(HIDDEN), ALU.mult, ALU.mult))
            done(v.tensor_tensor(bound[:, 7:8], bound[:, 6:7], bound[:, 7:8], ALU.add))
            done(v.tensor_tensor(bound[:, 7:8], bound[:, 7:8], bound[:, 5:6], ALU.add))
            done(v.tensor_scalar(safe_flag[:, 0:1], bound[:, 7:8], FINITE_BOUND, None, ALU.is_le))
            safe = dve.value_load(safe_flag[0:1, 0:1], min_val=0, max_val=1)
            dve.wait_ge(pe_pro, 7)
            v.tensor_copy(o_scale_bc[:, :], bank[6][:, :]).then_inc(o_scale_ready, 1)
            dve.wait_ge(pe_pro, 8)
            for b in range(2):
                v.tensor_copy(convb_bc[:, b * HIDDEN:(b + 1) * HIDDEN], bank[5 + 2 * b][:, :]).then_inc(convb_ready, 1)



            def nan_to_num(y, steps, n):
                width = y.shape[1]
                low, high, fin = g_low[:, 0:width], g_high[:, 0:width], g_fin[:, 0:width]
                v.tensor_scalar(low, y, -NAN_LIMIT, NAN_LIMIT, ALU.max, ALU.min).then_inc(steps[0], 1)
                v.tensor_scalar(high, y, NAN_LIMIT, -NAN_LIMIT, ALU.min, ALU.max).then_inc(steps[1], 1)
                v.tensor_scalar(fin, y, 0.0, 0.0, ALU.mult, ALU.is_equal).then_inc(steps[2], 1)
                dve.wait_ge(steps[0], n)
                dve.wait_ge(steps[1], n)
                v.tensor_tensor(low, low, high, ALU.add).then_inc(steps[3], 1)
                dve.wait_ge(steps[3], n)
                v.tensor_scalar(low, low, 0.5, None, ALU.mult).then_inc(steps[4], 1)
                wait_apart(dve, steps[4], n)
                wait_apart(dve, steps[2], n)
                v.copy_predicated(low, fin, y).then_inc(steps[5], 1)
                dve.wait_ge(steps[5], n)
                return v.tensor_copy(y, low)

            with dve.Fori(1, PAIRS) as i:
                full_mixed(i)
                low_part(i)
            dve.wait_ge(qkv_copied, BLOCKS * PAIRS)
            with dve.If(safe == 1):
                v.memset(g_low[:, 0:1], 0.0).then_inc(qkv_guarded, 1)
            with dve.Else():
                for n in range(BLOCKS):
                    last = nan_to_num(qkv[:, n, :], qkv_guard, n + 1)
                    if n < BLOCKS - 1:
                        last.then_inc(qkv_guard[6], 1)
                        dve.wait_ge(qkv_guard[6], n + 1)
                    else:
                        last.then_inc(qkv_guarded, 1)
            dve.wait_ge(qkv_guarded, 1)
            v.transpose(values_t[:, :, :].rearrange("p b d -> p (b d)"), qkv[:, MEMBERS + 1, :]).then_inc(values_turned, 1)
            dve.wait_ge(values_turned, 1)
            dve.wait_ge(pool_const, 4)

            def spread_values(t):
                reached(dve, attn_done, t)
                for r in range(PER_TILE):
                    rows = slice(TOKENS * r, TOKENS * (r + 1))
                    src = values_t[rows, cols(t, PER_TILE), :].rearrange("p s (a d) -> p s a d", a=2)
                    dst = vals_diag[rows, :, :, 2 * DIM * r:2 * DIM * (r + 1)].rearrange("p s a (c d) -> p s a c d", c=2)
                    for a in range(2):
                        v.tensor_copy(dst[:, :, a, a, :], src[:, :, a, :]).then_inc(values_spread, 1)

            def softmax_shift(t):
                for h in range(2):
                    scores = ps_scores[h][:, :].rearrange("p (g k) -> p g k", k=TOKENS)
                    dve.wait_ge(scores_done, 2 * t + h + 1)
                    v.tensor_reduce(row_max[:, h, :], scores, AX_X, ALU.max).then_inc(max_ready, 1)
                    dve.wait_ge(max_ready, 2 * t + h + 1)
                    reached(dve, probs_ready, 2 * t)
                    v.tensor_tensor(probs[:, h, :, :], scores,
                                    row_max[:, h, :].unsqueeze(2).to_broadcast([P, HALF, TOKENS]),
                                    ALU.subtract).then_inc(shifted, 1)

            def softmax_sum(t, h):
                dve.wait_ge(exp_ready, 2 * t + h + 1)
                v.tensor_reduce(row_sum[:, h, :], probs[:, h, :, :], AX_X, ALU.add).then_inc(sum_ready, 1)
                dve.wait_ge(sum_ready, 2 * t + h + 1)
                v.reciprocal(row_inv[:, h, :], row_sum[:, h, :]).then_inc(inv_ready, 1)

            def attn_low(t):
                dve.wait_ge(attn_hi_ready, t + 1)
                reached(dve, y_done, t)
                v.tensor_tensor(attn_lo[:, :, :, :].rearrange("p j s q -> p s j q"), attn_view,
                                attn_hi[:, :, :, :].rearrange("p j s q -> p s j q").bitcast(F32),
                                ALU.subtract).then_inc(attn_lo_ready, 1)

            def scale_y(t):
                wait_apart(dve, y_done, t + 1)
                reached(dve, x1_ready, t)
                with dve.If(safe == 1):
                    v.tensor_tensor(o_out[:, :], ps_y[:, :], o_scale_bc[:, :], ALU.mult).then_inc(y_scaled, 1)
                with dve.Else():
                    v.tensor_tensor(o_out[:, :], ps_y[:, :], o_scale_bc[:, :], ALU.mult).then_inc(o_guard[6], 1)
                    dve.wait_ge(o_guard[6], t + 1)
                    nan_to_num(o_out[:, :], o_guard, t + 1).then_inc(y_scaled, 1)

            def bias_conv(t):
                dve.wait_ge(conv_done, t + 1)
                reached(dve, ffn_in_done, t)
                bias = convb_bc[:, cols(t, P)].rearrange("p (s o) -> p s o", o=TOKENS)
                v.tensor_tensor(convT[:, :, :, :].rearrange("p a s o -> p s a o"), ps_conv[:, :].rearrange("p (s a o) -> p s a o", s=PER_TILE, a=PHASES),
                                bias.unsqueeze(2).to_broadcast([P, PER_TILE, PHASES, TOKENS]),
                                ALU.add).then_inc(conv_biased, 1)

            def gate(u):
                def then(ins, ready):
                    ins.then_inc(ready, 1)
                    wait_apart(dve, ready, u + 1)

                dve.wait_ge(ffn_in_done, u + 1)
                then(v.tensor_tensor(logits[:, :], ps_ffn[:, EXPERTS * RANK:FFN_COLS], misc_sb[:, MISC["router_b"]],
                                     ALU.add), logits_ready)
                then(v.max(logit_top[:, :], logits[:, :]), top_ready)
                v.tensor_scalar(neg_max[:, :], logit_top[:, 0:1], -1.0, None, ALU.mult).then_inc(neg_max_ready, 1)
                wait_apart(dve, gate_exp, u + 1)
                then(v.max(gate_top[:, :], gate_e[:, :]), gate_top_ready)
                then(v.max_index(gate_idx[:, :], gate_top[:, :], gate_e[:, :]), gate_idx_ready)
                v.tensor_copy(gate_idx_f[:, :], gate_idx[:, 0:2]).then_inc(idx_f_ready, 1)
                then(v.tensor_tensor(gate_sum[:, :], gate_top[:, 0:1], gate_top[:, 1:2], ALU.add), gate_sum_ready)
                then(v.reciprocal(gate_inv[:, :], gate_sum[:, :]), gate_inv_ready)
                then(v.tensor_scalar(gate_two[:, :], gate_top[:, 0:2], gate_inv[:, :], None, ALU.mult), gate_two_ready)
                dve.wait_ge(idx_f_ready, u + 1)
                for n in range(2):
                    v.tensor_scalar(gate_w[:, n, :], misc_sb[:, MISC["iota"]], gate_idx_f[:, n:n + 1],
                                    gate_two[:, n:n + 1], ALU.is_equal, ALU.mult).then_inc(share_ready[n], 1)
                for n in range(2):
                    dve.wait_ge(share_ready[n], u + 1)
                then(v.tensor_tensor(gate_w[:, 2, :], gate_w[:, 0, :], gate_w[:, 1, :], ALU.add), gate_w_ready)
                reached(dve, gatedT_done, u)
                v.tensor_tensor(gated[:, :].rearrange("p (e r) -> p e r", r=RANK),
                                ps_ffn[:, 0:EXPERTS * RANK].rearrange("p (e r) -> p e r", r=RANK),
                                gate_w[:, 2, :].unsqueeze(2).to_broadcast([P, EXPERTS, RANK]),
                                ALU.mult).then_inc(gated_ready, 1)

            def finish(u):
                dve.wait_ge(ffn_done, u + 1)
                dve.wait_ge(x1_ready, u + 1)
                if isinstance(u, int):
                    dst, res = x1[:, u, :], x1[:, u, :]
                else:
                    dst = x1[:, bass.ds(u, 1), :].rearrange("p a n -> p (a n)")
                    res = x1[:, bass.ds(u, 1), :].rearrange("p a n -> p (a n)")
                v.scalar_tensor_tensor(out=dst, in0=ps_y[:, :], scalar=8.0 / RANK, in1=res, op0=ALU.mult,
                                       op1=ALU.add).then_inc(out_ready, 1)

            def tile_step(t, scores=True, conv=True, ffn=True):
                spread_values(t)
                if scores:
                    softmax_shift(t + 1)
                    softmax_sum(t + 1, 0)
                attn_low(t)
                if ffn:
                    finish(t - 2)
                if scores:
                    softmax_sum(t + 1, 1)
                if conv:
                    bias_conv(t - 1)
                scale_y(t)
                if conv:
                    gate(t - 1)

            dve.wait_ge(o_scale_ready, 1)
            dve.wait_ge(convb_ready, 2)
            softmax_shift(0)
            softmax_sum(0, 0)
            softmax_sum(0, 1)
            tile_step(0, conv=False, ffn=False)
            tile_step(1, ffn=False)
            with dve.Fori(2, TILES - 1) as t:
                tile_step(t)
            tile_step(TILES - 1, scores=False)
            finish(TILES - 2)
            bias_conv(TILES - 1)
            gate(TILES - 1)
            finish(TILES - 1)

        @block.tensor
        def _(pe):
            mm = nc.tensor.matmul
            pe.wait_ge(in_cond, 16)
            mm(bank[0][:, 0:SAMPLES], cond_sb[:, COND["W0"]], cond_sb[:, COND["condT"]], start=True,
               stop=True).then_inc(pe_pro, 1)
            pe.wait_ge(act_pro, 1)
            mm(bank[1][:, 0:SAMPLES], cond_sb[:, COND["W1"]], gelu0[:, :], start=True, stop=True).then_inc(pe_pro, 1)
            pe.wait_ge(dve_pro, 1)
            for t in range(TILES):
                last = mm(bank[2][:, t * MIXES:(t + 1) * MIXES],
                          gelu1_rep[:, t * PER_TILE:(t + 1) * PER_TILE, :], cond_sb[:, COND["W2"]],
                          start=True, stop=True)
            last.then_inc(pe_pro, 1)
            pe.wait_ge(dve_pro, 7)
            pe.wait_ge(in_misc, 16)
            nc.tensor.transpose(bank[3][0:TILES * MIXES, 0:P], att[:, :, :].rearrange("p t k -> p (t k)"),
                                ident).then_inc(pe_pro, 1)

            def mix(i):
                pe.wait_ge(in_pair, 16 * (i + 1))
                reached(pe, mixed_full, 2 * i)
                for b in range(2):
                    for ph in (2 * b, 2 * b + 1):
                        for a in range(2):
                            at = (ph % 2) * PAIR + a * P
                            if isinstance(i, int):
                                w = agg_diag[:, 2 * i + a, :, :].rearrange("p q o -> p (q o)")
                            else:
                                w = agg_diag[:, bass.ds(2 * i + a, 1), :, :].rearrange("p t q o -> p (t q o)")
                            last = mm(ps_mixed[b][:, at:at + P], x_pair[:, a, ph * STEPS:(ph + 1) * STEPS], w,
                                      start=True, stop=True)
                    last.then_inc(mixed_done, 1)

            pe.wait_ge(agg_ready, PER_TILE)
            mix(0)
            pe.wait_ge(dve_pro, 11)
            pe.wait_ge(pool_const, 1)
            for b in range(2):
                last = mm(bank[4 + b][:, :], ones[0:TILES * MIXES, :],
                          outer_b[:, :, :, :].rearrange("p t q o -> p (t q o)")[:, b * HIDDEN:(b + 1) * HIDDEN],
                          start=True, stop=True)
            last.then_inc(pe_pro, 1)
            pe.wait_ge(dve_pro, 19)
            pe.wait_ge(act_sums, BLOCKS + PHASES + 1)
            mm(bank[7][0:1, 0:4], ones[:, 0:1], sums[:, :], start=True, stop=True).then_inc(pe_pro, 1)
            mm(bank[6][:, :], ones[:, :], o_diag[:, :], start=True, stop=True).then_inc(pe_pro, 1)
            pe.wait_ge(outer_done, 1)
            pe.wait_ge(in_conv_b, 16)
            pe.wait_ge(dve_pro, 20)
            for b in range(2):
                half = slice(b * SAMPLES // 2, (b + 1) * SAMPLES // 2)
                mm(bank[5 + 2 * b][:, :], ones[:, :], outer[:, half, :].rearrange("p b o -> p (b o)"),
                   start=True, stop=False)
                last = mm(bank[5 + 2 * b][:, :].rearrange("p (b o) -> p b o", o=TOKENS), ones[0:1, :],
                          conv_b_sb[:, :].unsqueeze(1).to_broadcast([1, SAMPLES // 2, TOKENS]),
                          start=False, stop=True)
            last.then_inc(pe_pro, 1)

            def project(i, b):
                reached(pe, qkv_copied, BLOCKS * (i - 1) + 2 * (b + 1) if not isinstance(i, int) or i else 0)
                for n in (2 * b, 2 * b + 1):
                    dst = ps_qkv[b][:, (n % 2) * PAIR:(n % 2 + 1) * PAIR]
                    for ph in range(PHASES):
                        w = qkv_sign[:, ph, n * P:(n + 1) * P]
                        mm(dst, w, mixed_hi[:, ph, cols(i, PAIR)], start=(ph == 0), stop=False)
                        last = mm(dst, w, mixed_lo[:, ph, cols(i, PAIR)], start=False, stop=(ph == PHASES - 1))
                last.then_inc(qkv_done, 1)

            pe.wait_ge(act_sign, PHASES)
            pe.wait_ge(aggb_ready, 2)

            def pair_step(i, more=True):
                pe.wait_ge(hi_ready, 2 * (i + 1))
                pe.wait_ge(lo_ready, 2 * (i + 1))
                project(i, 0)
                if more:
                    mix(i + 1)
                project(i, 1)
                project(i, 2)

            pair_step(0)
            with pe.Fori(1, PAIRS - 1) as i:
                pair_step(i)
            pair_step(PAIRS - 1, more=False)

            def score(t):
                pe.wait_ge(q_staged, t + 1)
                pe.wait_ge(keys_spread, t + 1)
                reached(pe, shifted, 2 * t)
                for s in range(PER_TILE):
                    last = mm(ps_scores[s // 2][:, (s % 2) * PAIR:(s % 2 + 1) * PAIR],
                              q_tile[:, s, :, :],
                              keys_diag[:, s, :, :].rearrange("p g k -> p (g k)"), start=True, stop=True)
                    if s % 2:
                        last.then_inc(scores_done, 1)

            def turn_probs(t):
                for h in range(2):
                    pe.wait_ge(probs_ready, 2 * t + h + 1)
                    reached(pe, probsT_copied, 2 * t)
                    for s in (2 * h, 2 * h + 1):
                        for a in range(2):
                            at = ((s % 2) * 2 + a) * P
                            last = nc.tensor.transpose(ps_probsT[h][:, at:at + P], probs_n[:, s, PER_TILE * a:PER_TILE * (a + 1), :], ident)
                    last.then_inc(probsT_done, 1)

            def attend(t):
                pe.wait_ge(values_spread, 2 * PER_TILE * (t + 1))
                reached(pe, attn_lo_ready, t)
                for s in range(PER_TILE):
                    pe.wait_ge(probsT_copied, 2 * t + s // 2 + 1)
                    for a in range(2):
                        last = mm(ps_attn[:, s * P:(s + 1) * P], vals_diag[:, s, a, :], probsT[:, s, a, :],
                                  start=(a == 0), stop=(a == 1))
                last.then_inc(attn_done, 1)

            def project_out(t):
                pe.wait_ge(attn_hi_ready, t + 1)
                pe.wait_ge(attn_lo_ready, t + 1)
                reached(pe, y_scaled, t)
                reached(pe, out_ready, t - 1)
                for j in range(MEMBERS):
                    for part in (attn_hi, attn_lo):
                        last = mm(ps_y[:, :], part[:, j, :, :], wo_sign[:, j, :],
                                  start=(j == 0 and part is attn_hi), stop=(j == MEMBERS - 1 and part is attn_lo))
                last.then_inc(y_done, 1)

            def convolve(t):
                pe.wait_ge(phased, 16 * PHASED_DMAS * (t + 1))
                reached(pe, conv_biased, t)
                for s in range(PER_TILE):
                    for shift in range(3):
                        last = mm(ps_conv[:, s * P:(s + 1) * P], x1_phased[:, s, shift:shift + STEPS],
                                  conv_w_sb[:, shift, :], start=(shift == 0), stop=(shift == 2))
                last.then_inc(conv_done, 1)

            def ffn_up(t):
                pe.wait_ge(conv_biased, t + 1)
                reached(pe, gatedT_copied, t)
                for ph in range(PHASES):
                    last = mm(ps_ffn[:, 0:FFN_COLS], convT[:, ph, :, :], ffn_in_sb[:, ph, :],
                              start=(ph == 0), stop=(ph == PHASES - 1))
                last.then_inc(ffn_in_done, 1)

            def turn_gated(u):
                pe.wait_ge(gated_ready, u + 1)
                nc.tensor.transpose(ps_ffn[:, PAIR:PAIR + P], gated[:, :], ident).then_inc(gatedT_done, 1)

            def ffn_down(u):
                pe.wait_ge(gatedT_copied, u + 1)
                pe.wait_ge(y_scaled, u + 2 if not isinstance(u, int) else min(u + 2, TILES))
                reached(pe, out_ready, u)
                mm(ps_y[:, :], gatedT[:, :], ffn_out_sb[:, :], start=True, stop=True).then_inc(ffn_done, 1)

            def tile_step(t, scores=True, conv=True, ffn=True):
                turn_probs(t)
                if scores:
                    score(t + 1)
                if ffn:
                    turn_gated(t - 2)
                attend(t)
                if ffn:
                    ffn_down(t - 2)
                if conv:
                    convolve(t - 1)
                project_out(t)
                if conv:
                    ffn_up(t - 1)

            pe.wait_ge(qkv_copied, BLOCKS * PAIRS)
            pe.wait_ge(convb_ready, 2)
            pe.wait_ge(pool_const, 4)
            pe.wait_ge(in_ffn, 32)
            pe.wait_ge(in_conv, 16)
            score(0)
            pe.wait_ge(act_sign, PHASES + 1)
            tile_step(0, conv=False, ffn=False)
            tile_step(1, ffn=False)
            with pe.Fori(2, TILES - 1) as t:
                tile_step(t)
            tile_step(TILES - 1, scores=False)
            turn_gated(TILES - 2)
            ffn_down(TILES - 2)
            convolve(TILES - 1)
            ffn_up(TILES - 1)
            turn_gated(TILES - 1)
            ffn_down(TILES - 1)


def kernel(**inputs):
    import numpy as np
    import concourse.bacc as bacc
    from concourse.bass_utils import run_bass_kernel_spmd

    f = {k: np.asarray(a) for k, a in inputs.items()}
    dt = f["x"].dtype

    def phased(a):
        return np.ascontiguousarray(a.reshape(*a.shape[:-1], STEPS, PHASES).swapaxes(-1, -2)).reshape(a.shape)

    def head_order(a):
        return a.reshape(GROUPS, MEMBERS, DIM, *a.shape[1:]).swapaxes(0, 1).reshape(a.shape)

    def pack(widths, parts):
        cols_of, total = columns(widths)
        out = np.zeros((P, total), dt)
        for name, a in parts.items():
            out[:, cols_of[name]] = a
        return out

    cond_pack = pack(COND_COLS, dict(
        condT=f["cond_128"].T, W0=f["L0_cond_W0"], b0=f["L0_cond_b0"][:, None], W1=f["L0_cond_W1"],
        b1=f["L0_cond_b1"][:, None], W2=f["L0_cond_W2"], b2=f["L0_cond_b2"][None, :],
        cwT=f["L0_cond2_c_weight"].T))
    rows = np.arange(P)
    qkv_scale = np.concatenate([head_order(f["L0_attn_q_scale"]), f["L0_attn_k_scale"], f["L0_attn_v_scale"]])
    misc = pack(MISC_COLS, dict(
        ident=np.eye(P, dtype=dt), headmask=(rows[:, None] // DIM == np.arange(GROUPS).reshape(-1, 2).T.reshape(1, -1)),
        iota=np.arange(EXPERTS)[None, :], router_b=f["L0_ffn_router_b"][None, :],
        qkv_scale=qkv_scale.reshape(BLOCKS, P).T, o_scale=phased(f["L0_attn_o_scale"]).reshape(PHASES, P).T))
    mix_w = np.tile(f["L0_cond_weight"][..., 0].transpose(2, 1, 0), (PER_TILE, 1, 1))
    mix_b = np.zeros((TILES, MIXES, TILES, TOKENS), dt)
    for t in range(TILES):
        mix_b[t, :, t, :] = f["L0_cond_bias_k"]
    w_rows = np.concatenate([head_order(f["L0_attn_q_weight"]), f["L0_attn_k_weight"], f["L0_attn_v_weight"]])
    w_rows = phased(w_rows)
    qkvT = np.ascontiguousarray(w_rows.T).reshape(PHASES, P, BLOCKS * P)
    qkv_rows = w_rows.reshape(BLOCKS, P, HIDDEN).transpose(1, 0, 2)
    wo = phased(f["L0_attn_o_weight"].T)
    woT = head_order(wo).reshape(MEMBERS, P, HIDDEN).transpose(1, 0, 2)
    wo_rows = wo.T.reshape(PHASES, P, HIDDEN).transpose(1, 0, 2)
    w = f["L0_cond2_weight"]
    per_group = w.shape[1]
    conv_w = np.zeros((PHASES, TOKENS, 3, PHASES, TOKENS), dt)
    for shift in range(3):
        for src in range(PHASES):
            for dst in range(PHASES):
                tap = PHASES * (shift - 1) + src - dst + w.shape[2] // 2
                if 0 <= tap < w.shape[2]:
                    for o in range(TOKENS):
                        first = o // per_group * per_group
                        conv_w[src, first:first + per_group, shift, dst, o] = w[o, :, tap]
    ffn_in = np.concatenate([f["L0_ffn_A"].reshape(EXPERTS * RANK, HIDDEN), f["L0_ffn_router_w"]])
    ffn_in = phased(ffn_in).T.reshape(PHASES, P, FFN_COLS).transpose(1, 0, 2)
    ffn_out = phased(f["L0_ffn_Bm"].transpose(0, 2, 1).reshape(EXPERTS * RANK, HIDDEN))

    arrays = dict(
        cond_pack=cond_pack, misc=misc, mix_w=mix_w, mix_b=mix_b.reshape(TILES * MIXES, TILES, TOKENS),
        x_rows=phased(f["x"]).reshape(ROWS, HIDDEN), qkvT=qkvT, qkv_rows=qkv_rows, woT=woT, wo_rows=wo_rows,
        conv_w=conv_w.reshape(P, 3, P), conv_b=f["fside_S_0"][None, :], ffn_in=ffn_in, ffn_out=ffn_out)
    arrays = {k: np.ascontiguousarray(a) for k, a in arrays.items()}
    nc = bacc.Bacc("TRN2", target_bir_lowering=False, num_devices=1)
    args = {k: nc.dram_tensor(f"in_{k}", a.shape, mybir.dt.from_np(a.dtype), kind="ExternalInput").ap()
            for k, a in arrays.items()}
    out = nc.dram_tensor("out_rows", (ROWS, HIDDEN), F32, kind="ExternalOutput").ap()
    build(nc, out=out, **args)
    r = run_bass_kernel_spmd(nc, [{f"in_{k}": a for k, a in arrays.items()}], core_ids=[0])
    got = r.results[0]["out_rows"]
    return got.reshape(SAMPLES, TOKENS, PHASES, STEPS).swapaxes(-1, -2).reshape(SAMPLES, TOKENS, HIDDEN)
```

```python
from contextlib import ExitStack

import concourse.bass as bass
from concourse import mybir

F32 = mybir.dt.float32
F32R = mybir.dt.float32r
I32 = mybir.dt.int32
U32 = mybir.dt.uint32
ALU = mybir.AluOpType
ACT = mybir.ActivationFunctionType
AX_X = mybir.AxisListType.X

P = 128
SAMPLES, TOKENS, HIDDEN = 32, 32, 512
PHASES = 4
STEPS = HIDDEN // PHASES
PER_TILE = P // TOKENS
TILES = SAMPLES // PER_TILE
ROWS = SAMPLES * TOKENS
MIXES = 8
GROUPS, MEMBERS, DIM = 8, 4, 16
BLOCKS = MEMBERS + 2
EXPERTS, RANK = 8, 16
FFN_COLS = EXPERTS * RANK + EXPERTS
PAIR = 2 * P
PAIRS = ROWS // PAIR
HALF = 2 * GROUPS
NAN_LIMIT = 1e6
FINITE_BOUND = 1e37

COND_COLS = dict(condT=SAMPLES, W0=P, b0=1, W1=P, b1=1, W2=MIXES, b2=MIXES, cwT=TOKENS)
MISC_COLS = dict(ident=P, headmask=GROUPS, iota=EXPERTS, router_b=EXPERTS, qkv_scale=BLOCKS, o_scale=PHASES)


def columns(widths):
    at, out = 0, {}
    for name, w in widths.items():
        out[name] = slice(at, at + w)
        at += w
    return out, at


COND, COND_W = columns(COND_COLS)
MISC, MISC_W = columns(MISC_COLS)


def build(nc, cond_pack, misc, mix_w, mix_b, x_rows, qkvT, qkv_rows, woT, wo_rows, conv_w, conv_b,
          ffn_in, ffn_out, out):
    with ExitStack() as ctx:
        def sb(name, shape, dt=F32):
            return ctx.enter_context(nc.sbuf_tensor(name, shape, dt))

        def sem(name):
            return ctx.enter_context(nc.semaphore(name))

        cond_sb = sb("cond_sb", [P, COND_W])
        misc_sb = sb("misc_sb", [P, MISC_W])
        mix_w_sb = sb("mix_w_sb", [P, TOKENS, MIXES])
        mix_b_sb = sb("mix_b_sb", [TILES * MIXES, TILES, TOKENS])
        x_all = sb("x_all", [P, TILES, HIDDEN])
        x_pair = sb("x_pair", [P, 2, HIDDEN])
        qkvT_sb = sb("qkvT_sb", [P, PHASES, BLOCKS * P])
        woT_sb = sb("woT_sb", [P, MEMBERS, HIDDEN])
        rows_sb = sb("rows_sb", [P, BLOCKS + PHASES, HIDDEN])
        conv_w_sb = sb("conv_w_sb", [P, 3, P])
        conv_b_sb = sb("conv_b_sb", [1, TOKENS])
        ffn_in_sb = sb("ffn_in_sb", [P, PHASES, FFN_COLS])
        ffn_out_sb = sb("ffn_out_sb", [P, HIDDEN])
        ones = sb("ones", [P, P])
        gelu0 = sb("gelu0", [P, SAMPLES])
        gelu1 = sb("gelu1", [P, SAMPLES])
        att = sb("att", [P, TILES, MIXES])
        att_red = sb("att_red", [P, 2, TILES])
        attT = sb("attT", [TILES * MIXES, P])
        agg = sb("agg", [P, TILES, TOKENS])
        agg_diag = sb("agg_diag", [P, TILES, PER_TILE, TOKENS])
        aggb_bc = sb("aggb_bc", [P, ROWS])
        convb_bc = sb("convb_bc", [P, ROWS])
        scale_in = sb("scale_in", [P, BLOCKS + PHASES])
        scale_all = sb("scale_all", [P, BLOCKS + PHASES])
        o_scale_bc = sb("o_scale_bc", [P, HIDDEN])
        qkv_sign = sb("qkv_sign", [P, PHASES, BLOCKS * P], F32R)
        wo_sign = sb("wo_sign", [P, MEMBERS, HIDDEN], F32R)
        sums = sb("sums", [P, 4])
        bound = sb("bound", [1, 8])
        safe_flag = sb("safe_flag", [1, 2], I32)
        mixed = sb("mixed", [P, PHASES, PAIR])
        gelu1_rep = mixed[:, :, :].rearrange("p a n -> p (a n)").rearrange("p (b o) -> p b o", o=TOKENS)
        mixed_hi = sb("mixed_hi", [P, PHASES, ROWS], F32R)
        mixed_lo = sb("mixed_lo", [P, PHASES, ROWS], F32R)
        qkv = sb("qkv", [P, BLOCKS, ROWS])
        junk = qkv[:, 0:MEMBERS, :].rearrange("p b n -> p (b n)")
        prod = qkv[:, MEMBERS:, :].rearrange("p b (t k) -> p (b t) k", k=MIXES).rearrange("p (t o) k -> p t o k", t=TILES)
        values_t = sb("values_t", [P, SAMPLES, 2 * DIM])
        q_tile = sb("q_tile", [P, PER_TILE, MEMBERS, TOKENS])
        keys_diag = sb("keys_diag", [P, PER_TILE, GROUPS, TOKENS])
        vals_diag = sb("vals_diag", [P, PER_TILE, 2 * (P + DIM)])
        row_max = sb("row_max", [P, 2, HALF])
        probs = sb("probs", [P, 2, HALF, TOKENS])
        row_sum = sb("row_sum", [P, 2, HALF])
        row_inv = sb("row_inv", [P, 2, HALF])
        probs_n = sb("probs_n", [P, PER_TILE, GROUPS, TOKENS])
        outer_b = probs_n[0:TILES * MIXES, :, :, :].rearrange("p s g k -> p (s g) k").rearrange(
            "p (t q) o -> p t q o", q=PER_TILE)
        probsT = sb("probsT", [P, PER_TILE, 2, P])
        outer = probsT[:, :, :, :].rearrange("p s a n -> p (s a n)").rearrange("p (b o) -> p b o", o=TOKENS)
        attn_hi = sb("attn_hi", [P, MEMBERS, PER_TILE, TOKENS], F32R)
        attn_lo = sb("attn_lo", [P, MEMBERS, PER_TILE, TOKENS], F32R)
        o_out = sb("o_out", [P, HIDDEN])
        o_diag = o_out
        x1 = rows_sb[:, 0:TILES, :]
        x1_phased = sb("x1_phased", [P, PER_TILE, STEPS + 2])
        convT = sb("convT", [P, PHASES, PER_TILE, TOKENS])
        logit_top = sb("logit_top", [P, 8])
        neg_max = sb("neg_max", [P, 1])
        gate_idx = sb("gate_idx", [P, 8], U32)
        gate_idx_f = sb("gate_idx_f", [P, 2])
        gate_mask = sb("gate_mask", [P, 2, EXPERTS])
        gate_e = sb("gate_e", [P, 2])
        gate_sum = sb("gate_sum", [P, 1])
        gate_inv = sb("gate_inv", [P, 1])
        gate_w = sb("gate_w", [P, EXPERTS])
        gated = sb("gated", [P, P])
        gatedT = sb("gatedT", [P, P])
        g_low = rows_sb[:, TILES:, :].rearrange("p a n -> p (a n)")
        g_high = qkvT_sb[:, :, :].rearrange("p a n -> p (a n)")[:, 0:ROWS]
        g_fin = qkvT_sb[:, :, :].rearrange("p a n -> p (a n)")[:, ROWS:2 * ROWS].bitcast(I32)

        x1_dram = nc.dram_tensor("x1_turned", (ROWS, HIDDEN), F32, kind="Internal").ap()

        bank = [ctx.enter_context(nc.psum_tensor(f"bank{n}", [P, HIDDEN], F32)) for n in range(8)]
        ps_scores = bank[0:2]
        ps_probsT = bank[2:4]
        ps_attn, ps_y, ps_conv, ps_ffn = bank[4:8]
        attn_view = ps_attn[:, :].rearrange("p (s j q) -> p s j q", s=PER_TILE, j=MEMBERS)
        ps_mixed = bank[0:2]
        ps_qkv = bank[2:5]

        in_cond, in_misc, in_mix_w, in_mix_b = sem("in_cond"), sem("in_misc"), sem("in_mix_w"), sem("in_mix_b")
        in_pair, in_x = sem("in_pair"), sem("in_x")
        in_qkvT = [sem(f"in_qkvT{n}") for n in range(PHASES)]
        in_qkv_rows, in_wo_rows, in_woT = sem("in_qkv_rows"), sem("in_wo_rows"), sem("in_woT")
        in_conv_b, in_conv, in_ffn = sem("in_conv_b"), sem("in_conv"), sem("in_ffn")
        pool_const = sem("pool_const")
        pe_pro, dve_pro, act_pro = sem("pe_pro"), sem("dve_pro"), sem("act_pro")
        act_sign = sem("act_sign")
        act_sums = sem("act_sums")
        outer_done = sem("outer_done")
        agg_ready, aggb_ready, convb_ready = sem("agg_ready"), sem("aggb_ready"), sem("convb_ready")
        scale_ready, o_scale_ready = sem("scale_ready"), sem("o_scale_ready")
        mixed_done, mixed_full, hi_ready, lo_ready = sem("mixed_done"), sem("mixed_full"), sem("hi_ready"), sem("lo_ready")
        qkv_done, qkv_copied = sem("qkv_done"), sem("qkv_copied")
        qkv_guarded, values_turned = sem("qkv_guarded"), sem("values_turned")
        qkv_guard = [sem(f"qkv_guard{n}") for n in range(7)]
        o_guard = [sem(f"o_guard{n}") for n in range(7)]
        q_staged, keys_spread, values_spread = sem("q_staged"), sem("keys_spread"), sem("values_spread")
        scores_done, max_ready, shifted = sem("scores_done"), sem("max_ready"), sem("shifted")
        exp_ready, sum_ready, inv_ready = sem("exp_ready"), sem("sum_ready"), sem("inv_ready")
        probs_ready, probsT_done, probsT_copied = sem("probs_ready"), sem("probsT_done"), sem("probsT_copied")
        attn_done, attn_hi_ready, attn_lo_ready = sem("attn_done"), sem("attn_hi_ready"), sem("attn_lo_ready")
        y_done, y_scaled, x1_ready = sem("y_done"), sem("y_scaled"), sem("x1_ready")
        x1_stored = sem("x1_stored")
        phased, conv_done, conv_biased = sem("phased"), sem("conv_done"), sem("conv_biased")
        ffn_in_done, gate_exp, gated_ready = sem("ffn_in_done"), sem("gate_exp"), sem("gated_ready")
        top_ready, neg_max_ready, gate_idx_ready = sem("top_ready"), sem("neg_max_ready"), sem("gate_idx_ready")
        idx_f_ready, gate_mask_ready = sem("idx_f_ready"), sem("gate_mask_ready")
        gate_inv_ready, gate_w_ready = sem("gate_inv_ready"), sem("gate_w_ready")
        gatedT_done, gatedT_copied = sem("gatedT_done"), sem("gatedT_copied")
        ffn_done, out_ready, stored = sem("ffn_done"), sem("out_ready"), sem("stored")

        def reached(eng, s, n):
            if not isinstance(n, int) or n > 0:
                eng.wait_ge(s, n)

        ident = misc_sb[:, MISC["ident"]]

        def cols(i, width):
            return slice(i * width, (i + 1) * width) if isinstance(i, int) else bass.ds(i * width, width)

        def wait_apart(eng, s, n):
            if isinstance(n, int):
                eng.wait_ge(s, n)
            else:
                eng.wait_ge(s, 1)
                eng.wait_ge(s, n)

        block = ctx.enter_context(nc.Block())

        @block.sync
        def _(sp):
            pair_rows = x_rows.rearrange("(i a p) n -> i p a n", p=P, a=2)
            sp.dma_start(cond_sb[:, :], cond_pack).then_inc(in_cond, 16)
            sp.dma_start(mix_w_sb[:, :, :], mix_w).then_inc(in_mix_w, 16)
            sp.dma_start(misc_sb[:, :], misc).then_inc(in_misc, 16)
            sp.dma_start(x_pair[:, :, :], pair_rows[0]).then_inc(in_pair, 16)
            sp.dma_start(mix_b_sb[:, :, :], mix_b).then_inc(in_mix_b, 16)
            sp.dma_start(conv_b_sb[:, :], conv_b).then_inc(in_conv_b, 16)
            for n in range(PHASES):
                sp.dma_start(qkvT_sb[:, n, :], qkvT[n]).then_inc(in_qkvT[n], 16)
            sp.dma_start(rows_sb[:, 0:BLOCKS, :], qkv_rows).then_inc(in_qkv_rows, 16)
            sp.dma_start(rows_sb[:, BLOCKS:, :], wo_rows).then_inc(in_wo_rows, 16)
            sp.dma_start(x_all[:, :, :], x_rows.rearrange("(t p) n -> p t n", p=P)).then_inc(in_x, 16)
            sp.wait_ge(mixed_done, 2)
            sp.dma_start(x_pair[:, :, :], pair_rows[1]).then_inc(in_pair, 16)
            sp.dma_start(woT_sb[:, :, :], woT).then_inc(in_woT, 16)
            sp.dma_start(conv_w_sb[:, :, :], conv_w).then_inc(in_conv, 16)
            sp.dma_start(ffn_in_sb[:, :, :], ffn_in).then_inc(in_ffn, 16)
            sp.dma_start(ffn_out_sb[:, :], ffn_out).then_inc(in_ffn, 16)
            for i in range(2, PAIRS):
                sp.wait_ge(mixed_done, 2 * i)
                sp.dma_start(x_pair[:, :, :], pair_rows[i]).then_inc(in_pair, 16)

            out_rows = out.rearrange("(t p) n -> t p n", p=P)

            def store(u):
                sp.wait_ge(out_ready, u + 1)
                if isinstance(u, int):
                    sp.dma_start(out_rows[u], x1[:, u, :]).then_inc(stored, 16)
                else:
                    sp.dma_start(out[bass.ds(u * P, P), :], x1[:, bass.ds(u, 1), :].rearrange("p a n -> p (a n)")
                                 ).then_inc(stored, 16)

            def to_phases(t):
                sp.wait_ge(x1_ready, t + 1)
                if isinstance(t, int):
                    rows, src = x1_dram[t * P:(t + 1) * P, :], x1[:, t, :]
                else:
                    rows, src = x1_dram[bass.ds(t * P, P), :], x1[:, bass.ds(t, 1), :].rearrange("p a n -> p (a n)")
                sp.dma_start(rows, src).then_inc(x1_stored, 16)
                sp.wait_ge(x1_stored, 16 * (t + 1))
                reached(sp, conv_done, t)
                for ph in range(PHASES):
                    sp.dma_start(x1_phased[TOKENS * ph:TOKENS * (ph + 1), :, 1:1 + STEPS],
                                 rows[:, STEPS * ph:STEPS * (ph + 1)].rearrange("(s c) m -> c s m", c=TOKENS)
                                 ).then_inc(phased, 16)

            for t in range(3):
                to_phases(t)
            with sp.Fori(3, TILES) as t:
                store(t - 3)
                to_phases(t)
            for t in range(TILES - 3, TILES):
                store(t)
            sp.wait_ge(stored, 16 * TILES)

        @block.gpsimd
        def _(pool):
            pool.memset(ones[:, :], 1.0).then_inc(pool_const, 1)
            pool.memset(agg_diag[:, :, :, :], 0.0).then_inc(pool_const, 1)
            pool.memset(vals_diag[:, :, :], 0.0).then_inc(pool_const, 1)
            pool.memset(x1_phased[:, :, :], 0.0).then_inc(pool_const, 1)
            pool.wait_ge(in_cond, 16)
            pool.tensor_tensor(outer[:, :, :],
                               cond_sb[:, COND["condT"]].unsqueeze(2).to_broadcast([P, SAMPLES, TOKENS]),
                               cond_sb[:, COND["cwT"]].unsqueeze(1).to_broadcast([P, SAMPLES, TOKENS]),
                               ALU.mult).then_inc(outer_done, 1)

            def spread_keys(t):
                if isinstance(t, int) and t == 0:
                    pool.wait_ge(qkv_guarded, 1)
                    pool.wait_ge(in_misc, 16)
                reached(pool, scores_done, 2 * t)
                keys = qkv[:, MEMBERS, cols(t, P)].rearrange("p (s k) -> p s k", k=TOKENS)
                pool.tensor_tensor(keys_diag[:, :, :, :],
                                   keys.unsqueeze(2).to_broadcast([P, PER_TILE, GROUPS, TOKENS]),
                                   misc_sb[:, MISC["headmask"]].unsqueeze(1).unsqueeze(3)
                                   .to_broadcast([P, PER_TILE, GROUPS, TOKENS]),
                                   ALU.mult).then_inc(keys_spread, 1)

            def normalise(t):
                for h in range(2):
                    pool.wait_ge(inv_ready, 2 * t + h + 1)
                    reached(pool, probsT_done, 2 * t)
                    pool.tensor_tensor(probs_n[:, 2 * h:2 * h + 2, :, :].rearrange("p s g k -> p (s g) k"),
                                       probs[:, h, :, :],
                                       row_inv[:, h, :].unsqueeze(2).to_broadcast([P, HALF, TOKENS]),
                                       ALU.mult).then_inc(probs_ready, 1)

            def residual(t):
                pool.wait_ge(y_scaled, t + 1)
                if isinstance(t, int):
                    pool.tensor_tensor(x1[:, t, :], x_all[:, t, :], o_out[:, :], ALU.add).then_inc(x1_ready, 1)
                else:
                    pool.tensor_tensor(x1[:, bass.ds(t, 1), :].rearrange("p a n -> p (a n)"),
                                       x_all[:, bass.ds(t, 1), :].rearrange("p a n -> p (a n)"),
                                       o_out[:, :], ALU.add).then_inc(x1_ready, 1)

            spread_keys(0)
            pool.wait_ge(in_x, 16)
            spread_keys(1)
            normalise(0)
            with pool.Fori(0, TILES - 2) as t:
                spread_keys(t + 2)
                normalise(t + 1)
                residual(t)
            normalise(TILES - 1)
            residual(TILES - 2)
            residual(TILES - 1)

        @block.scalar
        def _(act):
            act.wait_ge(in_cond, 16)
            act.wait_ge(pe_pro, 1)
            nc.scalar.activation(gelu0[:, :], bank[0][:, 0:SAMPLES], ACT.Gelu,
                                 bias=cond_sb[:, COND["b0"]]).then_inc(act_pro, 1)
            act.wait_ge(pe_pro, 2)
            nc.scalar.activation(gelu1[:, :], bank[1][:, 0:SAMPLES], ACT.Gelu,
                                 bias=cond_sb[:, COND["b1"]]).then_inc(act_pro, 1)
            act.wait_ge(dve_pro, 4)
            nc.scalar.activation(att[:, :, :], att[:, :, :], ACT.Exp).then_inc(act_pro, 1)
            for n in range(PHASES):
                act.wait_ge(in_qkvT[n], 16)
                nc.scalar.activation(qkv_sign[:, n, :], qkvT_sb[:, n, :], ACT.Sign).then_inc(act_sign, 1)
            act.wait_ge(in_qkv_rows, 16)
            for n in range(BLOCKS + PHASES):
                if n == BLOCKS:
                    act.wait_ge(in_wo_rows, 16)
                nc.scalar.activation(junk[:, 0:HIDDEN], rows_sb[:, n, :], ACT.Abs,
                                     accum_out=scale_in[:, n:n + 1]).then_inc(act_sums, 1)
                act.wait_ge(act_sums, n + 1)
            act.wait_ge(in_x, 16)
            nc.scalar.activation(junk[:, :], x_all[:, :, :].rearrange("p t n -> p (t n)"), ACT.Abs,
                                 accum_out=sums[:, 0:1]).then_inc(act_sums, 1)

            def high_part(i):
                for b in range(2):
                    act.wait_ge(mixed_full, 2 * i + b + 1)
                    nc.scalar.activation(mixed_hi[:, 2 * b:2 * b + 2, cols(i, PAIR)],
                                         mixed[:, 2 * b:2 * b + 2, :], ACT.Copy).then_inc(hi_ready, 1)

            def scale_qkv(i):
                for b in range(3):
                    act.wait_ge(qkv_done, 3 * i + b + 1)
                    for n in (2 * b, 2 * b + 1):
                        nc.scalar.activation(qkv[:, n, cols(i, PAIR)],
                                             ps_qkv[b][:, (n % 2) * PAIR:(n % 2 + 1) * PAIR], ACT.Copy,
                                             scale=scale_all[:, n:n + 1]).then_inc(qkv_copied, 1)

            high_part(0)
            act.wait_ge(scale_ready, 1)
            with act.Fori(0, PAIRS - 1) as i:
                high_part(i + 1)
                scale_qkv(i)
            scale_qkv(PAIRS - 1)
            act.wait_ge(in_woT, 16)
            nc.scalar.activation(wo_sign[:, :, :], woT_sb[:, :, :], ACT.Sign).then_inc(act_sign, 1)

            def exponents(t):
                for h in range(2):
                    act.wait_ge(shifted, 2 * t + h + 1)
                    nc.scalar.activation(probs[:, h, :, :], probs[:, h, :, :], ACT.Exp,
                                         scale=float(DIM) ** -0.5).then_inc(exp_ready, 1)

            def copy_probsT(t):
                reached(act, attn_done, t)
                for h in range(2):
                    act.wait_ge(probsT_done, 2 * t + h + 1)
                    nc.scalar.activation(probsT[:, 2 * h:2 * h + 2, :, :].rearrange("p s a n -> p (s a n)"),
                                         ps_probsT[h][:, :], ACT.Copy).then_inc(probsT_copied, 1)

            def attn_high(t):
                act.wait_ge(attn_done, t + 1)
                reached(act, y_done, t)
                nc.scalar.activation(attn_hi[:, :, :, :].rearrange("p j s q -> p s j q"), attn_view, ACT.Copy).then_inc(attn_hi_ready, 1)

            def stage_queries(t):
                reached(act, scores_done, 2 * t)
                nc.scalar.activation(q_tile[:, :, :, :].rearrange("p s j q -> p j s q"),
                                     qkv[:, 0:MEMBERS, cols(t, P)].rearrange("p j (s q) -> p j s q", q=TOKENS),
                                     ACT.Copy).then_inc(q_staged, 1)

            def spread_values(t):
                reached(act, attn_done, t)
                for r in range(PER_TILE):
                    rows = slice(TOKENS * r, TOKENS * (r + 1))
                    src = values_t[rows, cols(t, PER_TILE), :].rearrange("p s (a d) -> p s a d", a=2)
                    dst = vals_diag[rows, :, :].rearrange("p s (a c) -> p s a c", a=2)
                    nc.scalar.activation(dst[:, :, :, 2 * DIM * r:2 * DIM * r + DIM], src,
                                         ACT.Copy).then_inc(values_spread, 1)

            def gate_exponents(u):
                act.wait_ge(neg_max_ready, u + 1)
                nc.scalar.activation(gate_e[:, :], logit_top[:, 0:2], ACT.Exp, bias=neg_max[:, :],
                                     accum_out=gate_sum[:, :]).then_inc(gate_exp, 1)

            def copy_gatedT(u):
                act.wait_ge(gatedT_done, u + 1)
                reached(act, ffn_done, u)
                nc.scalar.activation(gatedT[:, :], ps_ffn[:, PAIR:PAIR + P], ACT.Copy).then_inc(gatedT_copied, 1)

            def tile_step(t, ahead=2, gate=True):
                copy_probsT(t)
                if ahead >= 1:
                    exponents(t + 1)
                if ahead >= 2:
                    stage_queries(t + 2)
                attn_high(t)
                if ahead >= 1:
                    spread_values(t + 1)
                if gate:
                    gate_exponents(t - 2)
                    copy_gatedT(t - 2)

            act.wait_ge(qkv_guarded, 1)
            stage_queries(0)
            act.wait_ge(values_turned, 1)
            act.wait_ge(pool_const, 4)
            spread_values(0)
            stage_queries(1)
            exponents(0)
            tile_step(0, gate=False)
            tile_step(1, gate=False)
            with act.Fori(2, TILES - 2) as t:
                tile_step(t)
            tile_step(TILES - 2, ahead=1)
            tile_step(TILES - 1, ahead=0)
            gate_exponents(TILES - 2)
            copy_gatedT(TILES - 2)
            gate_exponents(TILES - 1)
            copy_gatedT(TILES - 1)

        @block.vector
        def _(dve):
            v = nc.vector
            count = [0]

            def done(ins):
                count[0] += 1
                ins.then_inc(dve_pro, 1)
                dve.wait_ge(dve_pro, count[0])

            dve.wait_ge(act_pro, 2)
            done(v.tensor_copy(gelu1_rep[:, :, :], gelu1[:, :].unsqueeze(2).to_broadcast([P, SAMPLES, TOKENS])))
            dve.wait_ge(pe_pro, 3)
            done(v.tensor_tensor(att[:, :, :], bank[2][:, 0:TILES * MIXES].rearrange("p (t k) -> p t k", k=MIXES),
                                 cond_sb[:, COND["b2"]].unsqueeze(1).to_broadcast([P, TILES, MIXES]), ALU.add))
            done(v.tensor_reduce(att_red[:, 0, :], att[:, :, :], AX_X, ALU.max))
            done(v.tensor_tensor(att[:, :, :], att[:, :, :],
                                 att_red[:, 0, :].unsqueeze(2).to_broadcast([P, TILES, MIXES]), ALU.subtract))
            dve.wait_ge(act_pro, 3)
            done(v.tensor_reduce(att_red[:, 0, :], att[:, :, :], AX_X, ALU.add))
            done(v.reciprocal(att_red[:, 1, :], att_red[:, 0, :]))
            done(v.tensor_tensor(att[:, :, :], att[:, :, :],
                                 att_red[:, 1, :].unsqueeze(2).to_broadcast([P, TILES, MIXES]), ALU.mult))
            dve.wait_ge(in_mix_w, 16)
            done(v.tensor_tensor(prod[:, :, :, :],
                                 att[:, :, :].unsqueeze(2).to_broadcast([P, TILES, TOKENS, MIXES]),
                                 mix_w_sb[:, :, :].unsqueeze(1).to_broadcast([P, TILES, TOKENS, MIXES]), ALU.mult))
            done(v.tensor_reduce(agg[:, :, :], prod[:, :, :, :], AX_X, ALU.add))
            dve.wait_ge(pool_const, 2)
            for q in range(PER_TILE):
                rows = slice(TOKENS * q, TOKENS * (q + 1))
                v.tensor_copy(agg_diag[rows, :, q, :], agg[rows, :, :]).then_inc(agg_ready, 1)
            dve.wait_ge(pe_pro, 4)
            done(v.tensor_copy(attT[:, :], bank[3][0:TILES * MIXES, 0:P]))
            dve.wait_ge(in_mix_b, 16)
            done(v.tensor_tensor(outer_b[:, :, :, :],
                                 attT[:, 0:P:TOKENS].unsqueeze(1).unsqueeze(3)
                                 .to_broadcast([TILES * MIXES, TILES, PER_TILE, TOKENS]),
                                 mix_b_sb[:, :, :].unsqueeze(2)
                                 .to_broadcast([TILES * MIXES, TILES, PER_TILE, TOKENS]), ALU.mult))
            dve.wait_ge(pe_pro, 5)
            for b in range(2):
                v.tensor_copy(aggb_bc[:, b * HIDDEN:(b + 1) * HIDDEN], bank[4 + b][:, :]).then_inc(aggb_ready, 1)

            def full_mixed(i):
                for b in range(2):
                    dve.wait_ge(mixed_done, 2 * i + b + 1)
                    reached(dve, lo_ready, 2 * i)
                    bias = aggb_bc[:, cols(i, PAIR)].unsqueeze(1).to_broadcast([P, 2, PAIR])
                    v.tensor_tensor(mixed[:, 2 * b:2 * b + 2, :],
                                    ps_mixed[b][:, :].rearrange("p (a n) -> p a n", a=2), bias,
                                    ALU.add).then_inc(mixed_full, 1)

            def low_part(i):
                for b in range(2):
                    dve.wait_ge(hi_ready, 2 * i + b + 1)
                    v.tensor_tensor(mixed_lo[:, 2 * b:2 * b + 2, cols(i, PAIR)], mixed[:, 2 * b:2 * b + 2, :],
                                    mixed_hi[:, 2 * b:2 * b + 2, cols(i, PAIR)].bitcast(F32),
                                    ALU.subtract).then_inc(lo_ready, 1)

            dve.wait_ge(aggb_ready, 2)
            full_mixed(0)
            low_part(0)

            dve.wait_ge(act_sums, BLOCKS + PHASES)
            dve.wait_ge(in_misc, 16)
            done(v.tensor_scalar(scale_in[:, :], scale_in[:, :], 1.0 / HIDDEN, 1e-8, ALU.mult, ALU.max))
            v.tensor_tensor(scale_all[:, 0:BLOCKS], scale_in[:, 0:BLOCKS], misc_sb[:, MISC["qkv_scale"]],
                            ALU.mult).then_inc(scale_ready, 1)
            v.tensor_tensor(scale_all[:, BLOCKS:], scale_in[:, BLOCKS:], misc_sb[:, MISC["o_scale"]],
                            ALU.mult).then_inc(scale_ready, 1)
            dve.wait_ge(scale_ready, 2)
            done(v.tensor_tensor(o_diag[:, :].rearrange("p (a n) -> p a n", a=PHASES),
                                 scale_all[:, BLOCKS:].unsqueeze(2).to_broadcast([P, PHASES, P]),
                                 ident.unsqueeze(1).to_broadcast([P, PHASES, P]), ALU.mult))
            for n, values in ((1, agg[:, :, :].rearrange("p t o -> p (t o)")), (2, aggb_bc[:, :]), (3, scale_all[:, :])):
                scratch = g_low[:, 0:values.shape[1]]
                done(v.scalar_tensor_tensor(out=scratch, in0=values, scalar=-1.0, in1=values, op0=ALU.mult,
                                            op1=ALU.max))
                done(v.tensor_reduce(sums[:, n:n + 1], scratch, AX_X, ALU.add))
            dve.wait_ge(pe_pro, 6)
            done(v.tensor_copy(bound[:, 0:4], bank[7][0:1, 0:4]))
            done(v.scalar_tensor_tensor(out=bound[:, 4:5], in0=bound[:, 0:1], scalar=bound[:, 1:2], in1=bound[:, 2:3],
                                        op0=ALU.mult, op1=ALU.add))
            done(v.tensor_scalar(bound[:, 5:6], bound[:, 4:5], bound[:, 3:4], float(HIDDEN), ALU.mult, ALU.mult))
            done(v.tensor_scalar(bound[:, 6:7], bound[:, 5:6], bound[:, 5:6], 4.0 * DIM, ALU.mult, ALU.mult))
            done(v.tensor_scalar(bound[:, 7:8], bound[:, 5:6], bound[:, 3:4], float(HIDDEN), ALU.mult, ALU.mult))
            done(v.tensor_tensor(bound[:, 7:8], bound[:, 6:7], bound[:, 7:8], ALU.add))
            done(v.tensor_tensor(bound[:, 7:8], bound[:, 7:8], bound[:, 5:6], ALU.add))
            done(v.tensor_scalar(safe_flag[:, 0:1], bound[:, 7:8], FINITE_BOUND, None, ALU.is_le))
            safe = dve.value_load(safe_flag[0:1, 0:1], min_val=0, max_val=1)
            dve.wait_ge(pe_pro, 7)
            v.tensor_copy(o_scale_bc[:, :], bank[6][:, :]).then_inc(o_scale_ready, 1)
            dve.wait_ge(pe_pro, 8)
            for b in range(2):
                v.tensor_copy(convb_bc[:, b * HIDDEN:(b + 1) * HIDDEN], bank[5 + 2 * b][:, :]).then_inc(convb_ready, 1)



            def nan_to_num(y, steps, n):
                width = y.shape[1]
                low, high, fin = g_low[:, 0:width], g_high[:, 0:width], g_fin[:, 0:width]
                v.tensor_scalar(low, y, -NAN_LIMIT, NAN_LIMIT, ALU.max, ALU.min).then_inc(steps[0], 1)
                v.tensor_scalar(high, y, NAN_LIMIT, -NAN_LIMIT, ALU.min, ALU.max).then_inc(steps[1], 1)
                v.tensor_scalar(fin, y, 0.0, 0.0, ALU.mult, ALU.is_equal).then_inc(steps[2], 1)
                dve.wait_ge(steps[0], n)
                dve.wait_ge(steps[1], n)
                v.tensor_tensor(low, low, high, ALU.add).then_inc(steps[3], 1)
                dve.wait_ge(steps[3], n)
                v.tensor_scalar(low, low, 0.5, None, ALU.mult).then_inc(steps[4], 1)
                wait_apart(dve, steps[4], n)
                wait_apart(dve, steps[2], n)
                v.copy_predicated(low, fin, y).then_inc(steps[5], 1)
                dve.wait_ge(steps[5], n)
                return v.tensor_copy(y, low)

            with dve.Fori(1, PAIRS) as i:
                full_mixed(i)
                low_part(i)
            dve.wait_ge(qkv_copied, BLOCKS * PAIRS)
            with dve.If(safe == 1):
                v.memset(g_low[:, 0:1], 0.0).then_inc(qkv_guarded, 1)
            with dve.Else():
                for n in range(BLOCKS):
                    last = nan_to_num(qkv[:, n, :], qkv_guard, n + 1)
                    if n < BLOCKS - 1:
                        last.then_inc(qkv_guard[6], 1)
                        dve.wait_ge(qkv_guard[6], n + 1)
                    else:
                        last.then_inc(qkv_guarded, 1)
            dve.wait_ge(qkv_guarded, 1)
            v.transpose(values_t[:, :, :].rearrange("p b d -> p (b d)"), qkv[:, MEMBERS + 1, :]).then_inc(values_turned, 1)

            def softmax_shift(t, h):
                scores = ps_scores[h][:, :].rearrange("p (g k) -> p g k", k=TOKENS)
                dve.wait_ge(scores_done, 2 * t + h + 1)
                v.tensor_reduce(row_max[:, h, :], scores, AX_X, ALU.max).then_inc(max_ready, 1)
                dve.wait_ge(max_ready, 2 * t + h + 1)
                reached(dve, probs_ready, 2 * t)
                v.tensor_tensor(probs[:, h, :, :], scores,
                                row_max[:, h, :].unsqueeze(2).to_broadcast([P, HALF, TOKENS]),
                                ALU.subtract).then_inc(shifted, 1)

            def softmax_sum(t, h):
                dve.wait_ge(exp_ready, 2 * t + h + 1)
                v.tensor_reduce(row_sum[:, h, :], probs[:, h, :, :], AX_X, ALU.add).then_inc(sum_ready, 1)
                dve.wait_ge(sum_ready, 2 * t + h + 1)
                v.reciprocal(row_inv[:, h, :], row_sum[:, h, :]).then_inc(inv_ready, 1)

            def attn_low(t):
                dve.wait_ge(attn_hi_ready, t + 1)
                reached(dve, y_done, t)
                v.tensor_tensor(attn_lo[:, :, :, :].rearrange("p j s q -> p s j q"), attn_view,
                                attn_hi[:, :, :, :].rearrange("p j s q -> p s j q").bitcast(F32),
                                ALU.subtract).then_inc(attn_lo_ready, 1)

            def scale_y(t):
                wait_apart(dve, y_done, t + 1)
                reached(dve, x1_ready, t)
                with dve.If(safe == 1):
                    v.tensor_tensor(o_out[:, :], ps_y[:, :], o_scale_bc[:, :], ALU.mult).then_inc(y_scaled, 1)
                with dve.Else():
                    v.tensor_tensor(o_out[:, :], ps_y[:, :], o_scale_bc[:, :], ALU.mult).then_inc(o_guard[6], 1)
                    dve.wait_ge(o_guard[6], t + 1)
                    nan_to_num(o_out[:, :], o_guard, t + 1).then_inc(y_scaled, 1)

            def bias_conv(t):
                dve.wait_ge(conv_done, t + 1)
                reached(dve, ffn_in_done, t)
                bias = convb_bc[:, cols(t, P)].rearrange("p (s o) -> p s o", o=TOKENS)
                v.tensor_tensor(convT[:, :, :, :].rearrange("p a s o -> p s a o"), ps_conv[:, :].rearrange("p (s a o) -> p s a o", s=PER_TILE, a=PHASES),
                                bias.unsqueeze(2).to_broadcast([P, PER_TILE, PHASES, TOKENS]),
                                ALU.add).then_inc(conv_biased, 1)

            def gate_top(u):
                wait_apart(dve, ffn_in_done, u + 1)
                v.max(logit_top[:, :], ps_ffn[:, EXPERTS * RANK:FFN_COLS]).then_inc(top_ready, 1)
                wait_apart(dve, top_ready, u + 1)
                v.max_index(gate_idx[:, :], logit_top[:, :],
                            ps_ffn[:, EXPERTS * RANK:FFN_COLS]).then_inc(gate_idx_ready, 1)
                v.tensor_scalar(neg_max[:, :], logit_top[:, 0:1], -1.0, None, ALU.mult).then_inc(neg_max_ready, 1)

            def gate_masks(u):
                dve.wait_ge(gate_idx_ready, u + 1)
                v.tensor_copy(gate_idx_f[:, :], gate_idx[:, 0:2]).then_inc(idx_f_ready, 1)
                dve.wait_ge(idx_f_ready, u + 1)
                v.tensor_tensor(gate_mask[:, :, :],
                                misc_sb[:, MISC["iota"]].unsqueeze(1).to_broadcast([P, 2, EXPERTS]),
                                gate_idx_f[:, :].unsqueeze(2).to_broadcast([P, 2, EXPERTS]),
                                ALU.is_equal).then_inc(gate_mask_ready, 1)

            def gate_weights(u):
                dve.wait_ge(gate_exp, u + 1)
                v.reciprocal(gate_inv[:, :], gate_sum[:, :]).then_inc(gate_inv_ready, 1)
                dve.wait_ge(gate_mask_ready, u + 1)
                v.scalar_tensor_tensor(out=gate_w[:, :], in0=gate_mask[:, 1, :], scalar=gate_e[:, 1:2],
                                       in1=gate_mask[:, 0, :], op0=ALU.mult, op1=ALU.add).then_inc(gate_w_ready, 1)

            def gate_apply(u):
                dve.wait_ge(gate_w_ready, u + 1)
                dve.wait_ge(gate_inv_ready, u + 1)
                reached(dve, gatedT_done, u)
                v.scalar_tensor_tensor(out=gated[:, :].rearrange("p (e r) -> p e r", r=RANK),
                                       in0=ps_ffn[:, 0:EXPERTS * RANK].rearrange("p (e r) -> p e r", r=RANK),
                                       scalar=gate_inv[:, :],
                                       in1=gate_w[:, :].unsqueeze(2).to_broadcast([P, EXPERTS, RANK]),
                                       op0=ALU.mult, op1=ALU.mult).then_inc(gated_ready, 1)

            def finish(u):
                dve.wait_ge(ffn_done, u + 1)
                dve.wait_ge(x1_ready, u + 1)
                if isinstance(u, int):
                    dst, res = x1[:, u, :], x1[:, u, :]
                else:
                    dst = x1[:, bass.ds(u, 1), :].rearrange("p a n -> p (a n)")
                    res = x1[:, bass.ds(u, 1), :].rearrange("p a n -> p (a n)")
                v.scalar_tensor_tensor(out=dst, in0=ps_y[:, :], scalar=8.0 / RANK, in1=res, op0=ALU.mult,
                                       op1=ALU.add).then_inc(out_ready, 1)

            def tile_step(t, scores=True, up=True, down=True):
                if up:
                    bias_conv(t - 2)
                if down:
                    finish(t - 3)
                if scores:
                    softmax_shift(t + 1, 0)
                    softmax_shift(t + 1, 1)
                attn_low(t)
                if scores:
                    softmax_sum(t + 1, 0)
                if up:
                    gate_top(t - 2)
                if scores:
                    softmax_sum(t + 1, 1)
                if up:
                    gate_masks(t - 2)
                    gate_weights(t - 2)
                scale_y(t)
                if up:
                    gate_apply(t - 2)

            dve.wait_ge(o_scale_ready, 1)
            dve.wait_ge(convb_ready, 2)
            softmax_shift(0, 0)
            softmax_shift(0, 1)
            softmax_sum(0, 0)
            softmax_sum(0, 1)
            tile_step(0, up=False, down=False)
            tile_step(1, up=False, down=False)
            tile_step(2, down=False)
            with dve.Fori(3, TILES - 1) as t:
                tile_step(t)
            tile_step(TILES - 1, scores=False)
            bias_conv(TILES - 2)
            finish(TILES - 3)
            for u in (TILES - 2, TILES - 1):
                if u == TILES - 1:
                    bias_conv(u)
                gate_top(u)
                gate_masks(u)
                gate_weights(u)
                gate_apply(u)
                finish(u)

        @block.tensor
        def _(pe):
            mm = nc.tensor.matmul
            pe.wait_ge(in_cond, 16)
            mm(bank[0][:, 0:SAMPLES], cond_sb[:, COND["W0"]], cond_sb[:, COND["condT"]], start=True,
               stop=True).then_inc(pe_pro, 1)
            pe.wait_ge(act_pro, 1)
            mm(bank[1][:, 0:SAMPLES], cond_sb[:, COND["W1"]], gelu0[:, :], start=True, stop=True).then_inc(pe_pro, 1)
            pe.wait_ge(dve_pro, 1)
            for t in range(TILES):
                last = mm(bank[2][:, t * MIXES:(t + 1) * MIXES],
                          gelu1_rep[:, t * PER_TILE:(t + 1) * PER_TILE, :], cond_sb[:, COND["W2"]],
                          start=True, stop=True)
            last.then_inc(pe_pro, 1)
            pe.wait_ge(dve_pro, 7)
            pe.wait_ge(in_misc, 16)
            nc.tensor.transpose(bank[3][0:TILES * MIXES, 0:P], att[:, :, :].rearrange("p t k -> p (t k)"),
                                ident).then_inc(pe_pro, 1)

            def mix(i):
                pe.wait_ge(in_pair, 16 * (i + 1))
                reached(pe, mixed_full, 2 * i)
                for b in range(2):
                    for ph in (2 * b, 2 * b + 1):
                        for a in range(2):
                            at = (ph % 2) * PAIR + a * P
                            if isinstance(i, int):
                                w = agg_diag[:, 2 * i + a, :, :].rearrange("p q o -> p (q o)")
                            else:
                                w = agg_diag[:, bass.ds(2 * i + a, 1), :, :].rearrange("p t q o -> p (t q o)")
                            last = mm(ps_mixed[b][:, at:at + P], x_pair[:, a, ph * STEPS:(ph + 1) * STEPS], w,
                                      start=True, stop=True)
                    last.then_inc(mixed_done, 1)

            pe.wait_ge(agg_ready, PER_TILE)
            mix(0)
            pe.wait_ge(dve_pro, 11)
            pe.wait_ge(pool_const, 1)
            for b in range(2):
                last = mm(bank[4 + b][:, :], ones[0:TILES * MIXES, :],
                          outer_b[:, :, :, :].rearrange("p t q o -> p (t q o)")[:, b * HIDDEN:(b + 1) * HIDDEN],
                          start=True, stop=True)
            last.then_inc(pe_pro, 1)
            pe.wait_ge(dve_pro, 19)
            pe.wait_ge(act_sums, BLOCKS + PHASES + 1)
            mm(bank[7][0:1, 0:4], ones[:, 0:1], sums[:, :], start=True, stop=True).then_inc(pe_pro, 1)
            mm(bank[6][:, :], ones[:, :], o_diag[:, :], start=True, stop=True).then_inc(pe_pro, 1)
            pe.wait_ge(outer_done, 1)
            pe.wait_ge(in_conv_b, 16)
            pe.wait_ge(dve_pro, 20)
            for b in range(2):
                half = slice(b * SAMPLES // 2, (b + 1) * SAMPLES // 2)
                mm(bank[5 + 2 * b][:, :], ones[:, :], outer[:, half, :].rearrange("p b o -> p (b o)"),
                   start=True, stop=False)
                last = mm(bank[5 + 2 * b][:, :].rearrange("p (b o) -> p b o", o=TOKENS), ones[0:1, :],
                          conv_b_sb[:, :].unsqueeze(1).to_broadcast([1, SAMPLES // 2, TOKENS]),
                          start=False, stop=True)
            last.then_inc(pe_pro, 1)

            def project(i, b):
                reached(pe, qkv_copied, BLOCKS * (i - 1) + 2 * (b + 1) if not isinstance(i, int) or i else 0)
                for n in (2 * b, 2 * b + 1):
                    dst = ps_qkv[b][:, (n % 2) * PAIR:(n % 2 + 1) * PAIR]
                    for ph in range(PHASES):
                        w = qkv_sign[:, ph, n * P:(n + 1) * P]
                        mm(dst, w, mixed_hi[:, ph, cols(i, PAIR)], start=(ph == 0), stop=False)
                        last = mm(dst, w, mixed_lo[:, ph, cols(i, PAIR)], start=False, stop=(ph == PHASES - 1))
                last.then_inc(qkv_done, 1)

            pe.wait_ge(act_sign, PHASES)
            pe.wait_ge(aggb_ready, 2)

            def pair_step(i, more=True):
                pe.wait_ge(hi_ready, 2 * (i + 1))
                pe.wait_ge(lo_ready, 2 * (i + 1))
                project(i, 0)
                if more:
                    mix(i + 1)
                project(i, 1)
                project(i, 2)

            pair_step(0)
            with pe.Fori(1, PAIRS - 1) as i:
                pair_step(i)
            pair_step(PAIRS - 1, more=False)

            def score(t):
                pe.wait_ge(q_staged, t + 1)
                pe.wait_ge(keys_spread, t + 1)
                reached(pe, shifted, 2 * t)
                for s in range(PER_TILE):
                    last = mm(ps_scores[s // 2][:, (s % 2) * PAIR:(s % 2 + 1) * PAIR],
                              q_tile[:, s, :, :],
                              keys_diag[:, s, :, :].rearrange("p g k -> p (g k)"), start=True, stop=True)
                    if s % 2:
                        last.then_inc(scores_done, 1)

            def turn_probs(t):
                for h in range(2):
                    pe.wait_ge(probs_ready, 2 * t + h + 1)
                    reached(pe, probsT_copied, 2 * t)
                    for s in (2 * h, 2 * h + 1):
                        for a in range(2):
                            at = ((s % 2) * 2 + a) * P
                            last = nc.tensor.transpose(ps_probsT[h][:, at:at + P], probs_n[:, s, PER_TILE * a:PER_TILE * (a + 1), :], ident)
                    last.then_inc(probsT_done, 1)

            def attend(t):
                pe.wait_ge(values_spread, PER_TILE * (t + 1))
                reached(pe, attn_lo_ready, t)
                for s in range(PER_TILE):
                    pe.wait_ge(probsT_copied, 2 * t + s // 2 + 1)
                    for a in range(2):
                        last = mm(ps_attn[:, s * P:(s + 1) * P], vals_diag[:, s, a * P:(a + 1) * P], probsT[:, s, a, :],
                                  start=(a == 0), stop=(a == 1))
                last.then_inc(attn_done, 1)

            def project_out(t):
                pe.wait_ge(attn_hi_ready, t + 1)
                pe.wait_ge(attn_lo_ready, t + 1)
                reached(pe, y_scaled, t)
                reached(pe, out_ready, t - 2)
                for j in range(MEMBERS):
                    for part in (attn_hi, attn_lo):
                        last = mm(ps_y[:, :], part[:, j, :, :], wo_sign[:, j, :],
                                  start=(j == 0 and part is attn_hi), stop=(j == MEMBERS - 1 and part is attn_lo))
                last.then_inc(y_done, 1)

            def convolve(t):
                pe.wait_ge(phased, 16 * PHASES * (t + 1))
                reached(pe, conv_biased, t)
                for s in range(PER_TILE):
                    for shift in range(3):
                        last = mm(ps_conv[:, s * P:(s + 1) * P], x1_phased[:, s, shift:shift + STEPS],
                                  conv_w_sb[:, shift, :], start=(shift == 0), stop=(shift == 2))
                last.then_inc(conv_done, 1)

            def ffn_up(t):
                pe.wait_ge(conv_biased, t + 1)
                for ph in range(PHASES):
                    mm(ps_ffn[:, 0:FFN_COLS], convT[:, ph, :, :], ffn_in_sb[:, ph, :],
                              start=(ph == 0), stop=False)
                last = mm(ps_ffn[:, EXPERTS * RANK:FFN_COLS], ones[0:1, :], misc_sb[0:1, MISC["router_b"]],
                          start=False, stop=True)
                last.then_inc(ffn_in_done, 1)

            def turn_gated(u):
                pe.wait_ge(gated_ready, u + 1)
                reached(pe, gatedT_copied, u)
                nc.tensor.transpose(ps_ffn[:, PAIR:PAIR + P], gated[:, :], ident).then_inc(gatedT_done, 1)

            def ffn_down(u):
                pe.wait_ge(gatedT_copied, u + 1)
                pe.wait_ge(y_scaled, u + 3 if not isinstance(u, int) else min(u + 3, TILES))
                reached(pe, out_ready, u)
                mm(ps_y[:, :], gatedT[:, :], ffn_out_sb[:, :], start=True, stop=True).then_inc(ffn_done, 1)

            def tile_step(t, scores=True, conv=True, up=True, down=True):
                turn_probs(t)
                if down:
                    ffn_down(t - 3)
                if scores:
                    score(t + 1)
                attend(t)
                if up:
                    ffn_up(t - 2)
                project_out(t)
                if conv:
                    convolve(t - 1)
                if up:
                    turn_gated(t - 2)

            pe.wait_ge(qkv_copied, BLOCKS * PAIRS)
            pe.wait_ge(convb_ready, 2)
            pe.wait_ge(pool_const, 4)
            pe.wait_ge(in_ffn, 32)
            pe.wait_ge(in_conv, 16)
            score(0)
            pe.wait_ge(act_sign, PHASES + 1)
            tile_step(0, conv=False, up=False, down=False)
            tile_step(1, up=False, down=False)
            tile_step(2, down=False)
            with pe.Fori(3, TILES - 1) as t:
                tile_step(t)
            tile_step(TILES - 1, scores=False)
            ffn_down(TILES - 3)
            ffn_up(TILES - 2)
            convolve(TILES - 1)
            turn_gated(TILES - 2)
            ffn_down(TILES - 2)
            ffn_up(TILES - 1)
            turn_gated(TILES - 1)
            ffn_down(TILES - 1)


def kernel(**inputs):
    import numpy as np
    import concourse.bacc as bacc
    from concourse.bass_utils import run_bass_kernel_spmd

    f = {k: np.asarray(a) for k, a in inputs.items()}
    dt = f["x"].dtype

    def phased(a):
        return np.ascontiguousarray(a.reshape(*a.shape[:-1], STEPS, PHASES).swapaxes(-1, -2)).reshape(a.shape)

    def head_order(a):
        return a.reshape(GROUPS, MEMBERS, DIM, *a.shape[1:]).swapaxes(0, 1).reshape(a.shape)

    def pack(widths, parts):
        cols_of, total = columns(widths)
        out = np.zeros((P, total), dt)
        for name, a in parts.items():
            out[:, cols_of[name]] = a
        return out

    cond_pack = pack(COND_COLS, dict(
        condT=f["cond_128"].T, W0=f["L0_cond_W0"], b0=f["L0_cond_b0"][:, None], W1=f["L0_cond_W1"],
        b1=f["L0_cond_b1"][:, None], W2=f["L0_cond_W2"], b2=f["L0_cond_b2"][None, :],
        cwT=f["L0_cond2_c_weight"].T))
    rows = np.arange(P)
    qkv_scale = np.concatenate([head_order(f["L0_attn_q_scale"]), f["L0_attn_k_scale"], f["L0_attn_v_scale"]])
    misc = pack(MISC_COLS, dict(
        ident=np.eye(P, dtype=dt), headmask=(rows[:, None] // DIM == np.arange(GROUPS).reshape(-1, 2).T.reshape(1, -1)),
        iota=np.arange(EXPERTS)[None, :], router_b=f["L0_ffn_router_b"][None, :],
        qkv_scale=qkv_scale.reshape(BLOCKS, P).T, o_scale=phased(f["L0_attn_o_scale"]).reshape(PHASES, P).T))
    mix_w = np.tile(f["L0_cond_weight"][..., 0].transpose(2, 1, 0), (PER_TILE, 1, 1))
    mix_b = np.zeros((TILES, MIXES, TILES, TOKENS), dt)
    for t in range(TILES):
        mix_b[t, :, t, :] = f["L0_cond_bias_k"]
    w_rows = np.concatenate([head_order(f["L0_attn_q_weight"]), f["L0_attn_k_weight"], f["L0_attn_v_weight"]])
    w_rows = phased(w_rows)
    qkvT = np.ascontiguousarray(w_rows.T).reshape(PHASES, P, BLOCKS * P)
    qkv_rows = w_rows.reshape(BLOCKS, P, HIDDEN).transpose(1, 0, 2)
    wo = phased(f["L0_attn_o_weight"].T)
    woT = head_order(wo).reshape(MEMBERS, P, HIDDEN).transpose(1, 0, 2)
    wo_rows = wo.T.reshape(PHASES, P, HIDDEN).transpose(1, 0, 2)
    w = f["L0_cond2_weight"]
    per_group = w.shape[1]
    conv_w = np.zeros((PHASES, TOKENS, 3, PHASES, TOKENS), dt)
    for shift in range(3):
        for src in range(PHASES):
            for dst in range(PHASES):
                tap = PHASES * (shift - 1) + src - dst + w.shape[2] // 2
                if 0 <= tap < w.shape[2]:
                    for o in range(TOKENS):
                        first = o // per_group * per_group
                        conv_w[src, first:first + per_group, shift, dst, o] = w[o, :, tap]
    ffn_in = np.concatenate([f["L0_ffn_A"].reshape(EXPERTS * RANK, HIDDEN), f["L0_ffn_router_w"]])
    ffn_in = phased(ffn_in).T.reshape(PHASES, P, FFN_COLS).transpose(1, 0, 2)
    ffn_out = phased(f["L0_ffn_Bm"].transpose(0, 2, 1).reshape(EXPERTS * RANK, HIDDEN))

    arrays = dict(
        cond_pack=cond_pack, misc=misc, mix_w=mix_w, mix_b=mix_b.reshape(TILES * MIXES, TILES, TOKENS),
        x_rows=phased(f["x"]).reshape(ROWS, HIDDEN), qkvT=qkvT, qkv_rows=qkv_rows, woT=woT, wo_rows=wo_rows,
        conv_w=conv_w.reshape(P, 3, P), conv_b=f["fside_S_0"][None, :], ffn_in=ffn_in, ffn_out=ffn_out)
    arrays = {k: np.ascontiguousarray(a) for k, a in arrays.items()}
    nc = bacc.Bacc("TRN2", target_bir_lowering=False, num_devices=1)
    args = {k: nc.dram_tensor(f"in_{k}", a.shape, mybir.dt.from_np(a.dtype), kind="ExternalInput").ap()
            for k, a in arrays.items()}
    out = nc.dram_tensor("out_rows", (ROWS, HIDDEN), F32, kind="ExternalOutput").ap()
    build(nc, out=out, **args)
    r = run_bass_kernel_spmd(nc, [{f"in_{k}": a for k, a in arrays.items()}], core_ids=[0])
    got = r.results[0]["out_rows"]
    return got.reshape(SAMPLES, TOKENS, PHASES, STEPS).swapaxes(-1, -2).reshape(SAMPLES, TOKENS, HIDDEN)
```

```python
from contextlib import ExitStack

import concourse.bass as bass
from concourse import mybir
import numpy as np

F32 = mybir.dt.float32
F32R = mybir.dt.float32r
I32 = mybir.dt.int32
U32 = mybir.dt.uint32
ALU = mybir.AluOpType
ACT = mybir.ActivationFunctionType
AX_X = mybir.AxisListType.X

P = 128
SAMPLES, TOKENS, HIDDEN = 32, 32, 512
PHASES = 4
STEPS = HIDDEN // PHASES
PER_TILE = P // TOKENS
TILES = SAMPLES // PER_TILE
ROWS = SAMPLES * TOKENS
MIXES = 8
GROUPS, MEMBERS, DIM = 8, 4, 16
BLOCKS = MEMBERS + 2
EXPERTS, RANK = 8, 16
FFN_COLS = EXPERTS * RANK + EXPERTS
PAIR = 2 * P
PAIRS = ROWS // PAIR
HALF = 2 * GROUPS
NAN_LIMIT = 1e6
FINITE_BOUND = 1e37

COND_COLS = dict(condT=SAMPLES, W0=P, b0=1, W1=P, b1=1, W2=MIXES, b2=MIXES, cwT=TOKENS, conv_b=TOKENS,
                 spread=P, own_tile=TILES)
MISC_COLS = dict(ident=P, headmask=GROUPS, iota=EXPERTS, router_b=EXPERTS, qkv_scale=BLOCKS, o_scale=PHASES)


def columns(widths):
    at, out = 0, {}
    for name, w in widths.items():
        out[name] = slice(at, at + w)
        at += w
    return out, at


COND, COND_W = columns(COND_COLS)
MISC, MISC_W = columns(MISC_COLS)


def build(nc, cond_pack, misc, mix_w, mix_b, x_rows, qkvT, qkv_rows, woT, wo_rows, conv_w,
          ffn_in, ffn_out, out):
    with ExitStack() as ctx:
        def sb(name, shape, dt=F32):
            return ctx.enter_context(nc.sbuf_tensor(name, shape, dt))

        def sem(name):
            return ctx.enter_context(nc.semaphore(name))

        cond_sb = sb("cond_sb", [P, COND_W])
        misc_sb = sb("misc_sb", [P, MISC_W])
        mix_w_sb = sb("mix_w_sb", [P, TOKENS, MIXES])
        mix_b_sb = sb("mix_b_sb", [TILES * MIXES, TILES, TOKENS])
        x_all = sb("x_all", [P, TILES, HIDDEN])
        qkvT_sb = sb("qkvT_sb", [P, PHASES, BLOCKS * P])
        woT_sb = sb("woT_sb", [P, MEMBERS, HIDDEN])
        rows_sb = sb("rows_sb", [P, BLOCKS + PHASES, HIDDEN])
        conv_w_sb = sb("conv_w_sb", [P, 3, P])
        ffn_in_sb = sb("ffn_in_sb", [P, PHASES, FFN_COLS])
        ffn_out_sb = sb("ffn_out_sb", [P, HIDDEN])
        ones = sb("ones", [P, P])
        gelu0 = sb("gelu0", [P, SAMPLES])
        gelu1 = sb("gelu1", [P, SAMPLES])
        mix_top = sb("mix_top", [SAMPLES, 1])
        mix_e = sb("mix_e", [SAMPLES, MIXES])
        mix_sum = sb("mix_sum", [SAMPLES, 1])
        mix_inv = sb("mix_inv", [SAMPLES, 1])
        mix_own = sb("mix_own", [SAMPLES, TILES, MIXES])
        attT = sb("attT", [TILES * MIXES, PER_TILE])
        att_sb = sb("att_sb", [P, TILES * MIXES])
        prod = sb("prod", [P, 2, TOKENS, MIXES])
        agg = sb("agg", [P, TILES, TOKENS])
        agg_diag = sb("agg_diag", [P, TILES, PER_TILE, TOKENS])
        aggb_bc = sb("aggb_bc", [P, ROWS])
        convb_bc = sb("convb_bc", [P, ROWS])
        scale_in = sb("scale_in", [P, BLOCKS + PHASES])
        scale_all = sb("scale_all", [P, BLOCKS + PHASES])
        o_scale_bc = sb("o_scale_bc", [P, HIDDEN])
        qkv_sign = sb("qkv_sign", [P, PHASES, BLOCKS * P], F32R)
        wo_sign = sb("wo_sign", [P, MEMBERS, HIDDEN], F32R)
        table_load = sb("table_load", [P, 2])
        sums = sb("sums", [P, PAIRS + 3])
        bound = sb("bound", [1, PAIRS + 7])
        safe_flag = sb("safe_flag", [1, 2], I32)
        mixed = sb("mixed", [P, PHASES, PAIR])
        mixed_hi = sb("mixed_hi", [P, PHASES, ROWS], F32R)
        mixed_lo = sb("mixed_lo", [P, PHASES, ROWS], F32R)
        qkv = sb("qkv", [P, BLOCKS, ROWS])
        values_t = sb("values_t", [P, SAMPLES, 2 * DIM])
        q_tile = sb("q_tile", [P, PER_TILE, MEMBERS, TOKENS])
        keys_diag = sb("keys_diag", [P, PER_TILE, GROUPS, TOKENS])
        vals_diag = sb("vals_diag", [P, PER_TILE, 2, P // 2])
        row_max = sb("row_max", [P, 2, HALF])
        probs = sb("probs", [P, 2, HALF, TOKENS])
        junk = probs[:, :, :, :].rearrange("p h g k -> p (h g k)")
        row_sum = sb("row_sum", [P, 2, HALF])
        row_inv = sb("row_inv", [P, 2, HALF])
        probs_n = sb("probs_n", [P, PER_TILE, GROUPS, TOKENS])
        outer_b = probs_n[0:TILES * MIXES, :, :, :].rearrange("p s g k -> p (s g) k").rearrange(
            "p (t q) o -> p t q o", q=PER_TILE)
        probsT = sb("probsT", [P, PER_TILE, 2, P])
        outer = probsT[:, :, :, :].rearrange("p s a n -> p (s a n)").rearrange("p (b o) -> p b o", o=TOKENS)
        attn_hi = sb("attn_hi", [P, MEMBERS, PER_TILE, TOKENS], F32R)
        attn_lo = sb("attn_lo", [P, MEMBERS, PER_TILE, TOKENS], F32R)
        o_out = sb("o_out", [P, HIDDEN])
        o_diag = o_out
        x1 = rows_sb[:, 0:TILES, :]
        x1_phased = sb("x1_phased", [P, PER_TILE, STEPS + 2])
        convT = sb("convT", [P, PHASES, PER_TILE, TOKENS])
        logit_top = sb("logit_top", [P, 8])
        neg_max = sb("neg_max", [P, 1])
        gate_idx = sb("gate_idx", [P, 8], U32)
        gate_idx_f = sb("gate_idx_f", [P, 2])
        gate_mask = sb("gate_mask", [P, 2, EXPERTS])
        gate_e = sb("gate_e", [P, 2])
        gate_sum = sb("gate_sum", [P, 1])
        gate_inv = sb("gate_inv", [P, 1])
        gate_w = sb("gate_w", [P, EXPERTS])
        gated = sb("gated", [P, P])
        gatedT = sb("gatedT", [P, P])
        g_low = rows_sb[:, TILES:, :].rearrange("p a n -> p (a n)")
        g_high = qkvT_sb[:, :, :].rearrange("p a n -> p (a n)")[:, 0:ROWS]
        g_fin = qkvT_sb[:, :, :].rearrange("p a n -> p (a n)")[:, ROWS:2 * ROWS].bitcast(I32)

        x1_dram = nc.dram_tensor("x1_turned", (ROWS, HIDDEN), F32, kind="Internal").ap()

        bank = [ctx.enter_context(nc.psum_tensor(f"bank{n}", [P, HIDDEN], F32)) for n in range(8)]
        ps_probsT = bank[0:2]
        ps_y, ps_conv, ps_ffn, ps_attn = bank[2:6]
        ps_scores = bank[6:8]
        attn_view = ps_attn[:, :].rearrange("p (s j q) -> p s j q", s=PER_TILE, j=MEMBERS)
        ps_mixed = bank[0:2]
        ps_qkv = bank[2:5]
        ps_convb = bank[6:8]
        ps_aggb = (bank[5], bank[4])
        ps_bound, ps_o_scale = bank[7], bank[6]

        in_cond, in_misc, in_mix_w, in_mix_b = sem("in_cond"), sem("in_misc"), sem("in_mix_w"), sem("in_mix_b")
        in_pair = [sem(f"in_pair{n}") for n in range(PAIRS)]
        in_qkvT = [sem(f"in_qkvT{n}") for n in range(PHASES)]
        in_qkv_rows, in_wo_rows, in_woT = sem("in_qkv_rows"), sem("in_wo_rows"), sem("in_woT")
        in_conv, in_ffn = sem("in_conv"), sem("in_ffn")
        pool_const, table_ready = sem("pool_const"), sem("table_ready")
        cond_done, cond_gelu = sem("cond_done"), sem("cond_gelu")
        mix_top_ready, mix_shifted, mix_exp = sem("mix_top_ready"), sem("mix_shifted"), sem("mix_exp")
        mix_inv_ready, mix_own_ready = sem("mix_inv_ready"), sem("mix_own_ready")
        att_done, attT_ready, outer_b_ready = sem("att_done"), sem("attT_ready"), sem("outer_b_ready")
        att_kept = sem("att_kept")
        prod_ready, agg_summed, agg_ready = sem("prod_ready"), sem("agg_summed"), sem("agg_ready")
        aggb_done, aggb_ready = sem("aggb_done"), sem("aggb_ready")
        outer_done, convb_done, convb_ready = sem("outer_done"), sem("convb_done"), sem("convb_ready")
        act_sign, row_sums, x_sums = sem("act_sign"), sem("row_sums"), sem("x_sums")
        mean_ready, scale_ready, o_diag_ready = sem("mean_ready"), sem("scale_ready"), sem("o_diag_ready")
        o_scale_done, o_scale_ready = sem("o_scale_done"), sem("o_scale_ready")
        sums_ready, bound_done, bound_ready = sem("sums_ready"), sem("bound_done"), sem("bound_ready")
        mixed_done, mixed_full, hi_ready, lo_ready = sem("mixed_done"), sem("mixed_full"), sem("hi_ready"), sem("lo_ready")
        qkv_done, qkv_copied = sem("qkv_done"), sem("qkv_copied")
        qkv_guarded, values_turned = sem("qkv_guarded"), sem("values_turned")
        qkv_guard = [sem(f"qkv_guard{n}") for n in range(7)]
        o_guard = [sem(f"o_guard{n}") for n in range(7)]
        q_staged, keys_spread, values_spread = sem("q_staged"), sem("keys_spread"), sem("values_spread")
        scores_done, max_ready, shifted = sem("scores_done"), sem("max_ready"), sem("shifted")
        exp_ready, sum_ready, inv_ready = sem("exp_ready"), sem("sum_ready"), sem("inv_ready")
        probs_ready, probsT_done, probsT_copied = sem("probs_ready"), sem("probsT_done"), sem("probsT_copied")
        attn_done, attn_hi_ready, attn_lo_ready = sem("attn_done"), sem("attn_hi_ready"), sem("attn_lo_ready")
        y_done, y_scaled, x1_ready = sem("y_done"), sem("y_scaled"), sem("x1_ready")
        x1_stored = sem("x1_stored")
        phased, conv_done, conv_biased = sem("phased"), sem("conv_done"), sem("conv_biased")
        ffn_in_done, gate_exp, gated_ready = sem("ffn_in_done"), sem("gate_exp"), sem("gated_ready")
        top_ready, neg_max_ready, gate_idx_ready = sem("top_ready"), sem("neg_max_ready"), sem("gate_idx_ready")
        idx_f_ready, gate_mask_ready = sem("idx_f_ready"), sem("gate_mask_ready")
        gate_inv_ready, gate_w_ready = sem("gate_inv_ready"), sem("gate_w_ready")
        gatedT_done, gatedT_copied = sem("gatedT_done"), sem("gatedT_copied")
        ffn_done, out_ready, stored = sem("ffn_done"), sem("out_ready"), sem("stored")

        def reached(eng, s, n):
            if not isinstance(n, int) or n > 0:
                eng.wait_ge(s, n)

        ident = misc_sb[:, MISC["ident"]]

        def cols(i, width):
            return slice(i * width, (i + 1) * width) if isinstance(i, int) else bass.ds(i * width, width)

        def wait_apart(eng, s, n):
            if isinstance(n, int):
                eng.wait_ge(s, n)
            else:
                eng.wait_ge(s, 1)
                eng.wait_ge(s, n)

        block = ctx.enter_context(nc.Block())

        @block.sync
        def _(sp):
            pair_rows = x_rows.rearrange("(i a p) n -> i p a n", p=P, a=2)

            def load_pair(i):
                sp.dma_start(x_all[:, 2 * i:2 * i + 2, :], pair_rows[i]).then_inc(in_pair[i], 16)

            sp.dma_start(cond_sb[:, :], cond_pack).then_inc(in_cond, 16)
            sp.dma_start(mix_w_sb[:, :, :], mix_w).then_inc(in_mix_w, 16)
            sp.dma_start(mix_b_sb[:, :, :], mix_b).then_inc(in_mix_b, 16)
            load_pair(0)
            for n in range(PHASES):
                sp.dma_start(qkvT_sb[:, n, :], qkvT[n]).then_inc(in_qkvT[n], 16)
            sp.dma_start(misc_sb[:, :], misc).then_inc(in_misc, 16)
            sp.dma_start(rows_sb[:, 0:BLOCKS, :], qkv_rows).then_inc(in_qkv_rows, 16)
            load_pair(1)
            sp.dma_start(rows_sb[:, BLOCKS:, :], wo_rows).then_inc(in_wo_rows, 16)
            load_pair(2)
            load_pair(3)
            sp.dma_start(woT_sb[:, :, :], woT).then_inc(in_woT, 16)
            sp.dma_start(conv_w_sb[:, :, :], conv_w).then_inc(in_conv, 16)
            sp.dma_start(ffn_in_sb[:, :, :], ffn_in).then_inc(in_ffn, 16)
            sp.dma_start(ffn_out_sb[:, :], ffn_out).then_inc(in_ffn, 16)

            out_rows = out.rearrange("(t p) n -> t p n", p=P)

            def store(u):
                sp.wait_ge(out_ready, u + 1)
                if isinstance(u, int):
                    sp.dma_start(out_rows[u], x1[:, u, :]).then_inc(stored, 16)
                else:
                    sp.dma_start(out[bass.ds(u * P, P), :], x1[:, bass.ds(u, 1), :].rearrange("p a n -> p (a n)")
                                 ).then_inc(stored, 16)

            def to_phases(t):
                sp.wait_ge(x1_ready, t + 1)
                if isinstance(t, int):
                    rows, src = x1_dram[t * P:(t + 1) * P, :], x1[:, t, :]
                else:
                    rows, src = x1_dram[bass.ds(t * P, P), :], x1[:, bass.ds(t, 1), :].rearrange("p a n -> p (a n)")
                sp.dma_start(rows, src).then_inc(x1_stored, 16)
                sp.wait_ge(x1_stored, 16 * (t + 1))
                reached(sp, conv_done, t)
                for ph in range(PHASES):
                    sp.dma_start(x1_phased[TOKENS * ph:TOKENS * (ph + 1), :, 1:1 + STEPS],
                                 rows[:, STEPS * ph:STEPS * (ph + 1)].rearrange("(s c) m -> c s m", c=TOKENS)
                                 ).then_inc(phased, 16)

            for t in range(3):
                to_phases(t)
            with sp.Fori(3, TILES) as t:
                store(t - 3)
                to_phases(t)
            for t in range(TILES - 3, TILES):
                store(t)
            sp.wait_ge(stored, 16 * TILES)

        @block.gpsimd
        def _(pool):
            pool.memset(ones[:, :], 1.0).then_inc(pool_const, 1)
            pool.memset(agg_diag[:, :, :, :], 0.0).then_inc(pool_const, 1)
            pool.memset(vals_diag[:, :, :, :], 0.0).then_inc(pool_const, 1)
            pool.memset(x1_phased[:, :, :], 0.0).then_inc(pool_const, 1)
            pool.wait_ge(in_cond, 16)
            pool.tensor_tensor(outer[:, :, :],
                               cond_sb[:, COND["condT"]].unsqueeze(2).to_broadcast([P, SAMPLES, TOKENS]),
                               cond_sb[:, COND["cwT"]].unsqueeze(1).to_broadcast([P, SAMPLES, TOKENS]),
                               ALU.mult).then_inc(outer_done, 1)
            pool.wait_ge(in_mix_b, 16)
            pool.wait_ge(attT_ready, 1)
            for tiles in (slice(0, 2), slice(2, TILES)):
                n = tiles.stop - tiles.start
                pool.tensor_tensor(outer_b[:, tiles, :, :],
                                   attT[:, :].unsqueeze(1).unsqueeze(3)
                                   .to_broadcast([TILES * MIXES, n, PER_TILE, TOKENS]),
                                   mix_b_sb[:, tiles, :].unsqueeze(2)
                                   .to_broadcast([TILES * MIXES, n, PER_TILE, TOKENS]),
                                   ALU.mult).then_inc(outer_b_ready, 1)

            def spread_keys(t):
                if isinstance(t, int) and t == 0:
                    pool.wait_ge(qkv_guarded, 1)
                    pool.wait_ge(in_misc, 16)
                reached(pool, scores_done, 2 * t)
                keys = qkv[:, MEMBERS, cols(t, P)].rearrange("p (s k) -> p s k", k=TOKENS)
                pool.tensor_tensor(keys_diag[:, :, :, :],
                                   keys.unsqueeze(2).to_broadcast([P, PER_TILE, GROUPS, TOKENS]),
                                   misc_sb[:, MISC["headmask"]].unsqueeze(1).unsqueeze(3)
                                   .to_broadcast([P, PER_TILE, GROUPS, TOKENS]),
                                   ALU.mult).then_inc(keys_spread, 1)

            def normalise(t):
                for h in range(2):
                    pool.wait_ge(inv_ready, 2 * t + h + 1)
                    reached(pool, probsT_done, 2 * t)
                    pool.tensor_tensor(probs_n[:, 2 * h:2 * h + 2, :, :].rearrange("p s g k -> p (s g) k"),
                                       probs[:, h, :, :],
                                       row_inv[:, h, :].unsqueeze(2).to_broadcast([P, HALF, TOKENS]),
                                       ALU.mult).then_inc(probs_ready, 1)

            def residual(t):
                pool.wait_ge(y_scaled, t + 1)
                if isinstance(t, int):
                    pool.tensor_tensor(x1[:, t, :], x_all[:, t, :], o_out[:, :], ALU.add).then_inc(x1_ready, 1)
                else:
                    pool.tensor_tensor(x1[:, bass.ds(t, 1), :].rearrange("p a n -> p (a n)"),
                                       x_all[:, bass.ds(t, 1), :].rearrange("p a n -> p (a n)"),
                                       o_out[:, :], ALU.add).then_inc(x1_ready, 1)

            spread_keys(0)
            spread_keys(1)
            normalise(0)
            for i in range(PAIRS):
                pool.wait_ge(in_pair[i], 16)
            pool.wait_ge(qkv_guarded, PAIRS)
            with pool.Fori(0, TILES - 2) as t:
                spread_keys(t + 2)
                normalise(t + 1)
                residual(t)
            normalise(TILES - 1)
            residual(TILES - 2)
            residual(TILES - 1)

        @block.scalar
        def _(act):
            act.wait_ge(pool_const, 1)
            nc.scalar.activation(table_load[:, 0:1], ones[:, 0:1], ACT.Gelu).then_inc(table_ready, 1)
            act.wait_ge(in_cond, 16)
            act.wait_ge(cond_done, 1)
            nc.scalar.activation(gelu0[:, :], bank[0][:, 0:SAMPLES], ACT.Gelu,
                                 bias=cond_sb[:, COND["b0"]]).then_inc(cond_gelu, 1)
            act.wait_ge(cond_done, 2)
            nc.scalar.activation(gelu1[:, :], bank[1][:, 0:SAMPLES], ACT.Gelu,
                                 bias=cond_sb[:, COND["b1"]]).then_inc(cond_gelu, 1)
            nc.scalar.activation(table_load[:, 1:2], ones[:, 0:1], ACT.Exp).then_inc(table_ready, 1)
            act.wait_ge(mix_shifted, 1)
            nc.scalar.activation(mix_e[:, :], mix_e[:, :], ACT.Exp, accum_out=mix_sum[:, :]).then_inc(mix_exp, 1)
            for n in range(PHASES):
                act.wait_ge(in_qkvT[n], 16)
                nc.scalar.activation(qkv_sign[:, n, :], qkvT_sb[:, n, :], ACT.Sign).then_inc(act_sign, 1)

            def sum_rows(n):
                nc.scalar.activation(junk[:, 0:HIDDEN], rows_sb[:, n, :], ACT.Abs,
                                     accum_out=scale_in[:, n:n + 1]).then_inc(row_sums, 1)
                act.wait_ge(row_sums, n + 1)

            def sum_x(i):
                act.wait_ge(in_pair[i], 16)
                nc.scalar.activation(junk[:, :], x_all[:, 2 * i:2 * i + 2, :].rearrange("p t n -> p (t n)"), ACT.Abs,
                                     accum_out=sums[:, i:i + 1]).then_inc(x_sums, 1)
                act.wait_ge(x_sums, i + 1)

            def high_part(i):
                for b in range(2):
                    act.wait_ge(mixed_full, 2 * i + b + 1)
                    nc.scalar.activation(mixed_hi[:, 2 * b:2 * b + 2, cols(i, PAIR)],
                                         mixed[:, 2 * b:2 * b + 2, :], ACT.Copy).then_inc(hi_ready, 1)

            def scale_qkv(i, b):
                act.wait_ge(qkv_done, 3 * i + b + 1)
                for n in (2 * b, 2 * b + 1):
                    nc.scalar.activation(qkv[:, n, cols(i, PAIR)],
                                         ps_qkv[b][:, (n % 2) * PAIR:(n % 2 + 1) * PAIR], ACT.Copy,
                                         scale=scale_all[:, n:n + 1]).then_inc(qkv_copied, 1)

            def exponents(t, h):
                act.wait_ge(shifted, 2 * t + h + 1)
                nc.scalar.activation(probs[:, h, :, :], probs[:, h, :, :], ACT.Exp,
                                     scale=float(DIM) ** -0.5).then_inc(exp_ready, 1)

            def copy_probsT(t):
                reached(act, attn_done, t)
                for h in range(2):
                    act.wait_ge(probsT_done, 2 * t + h + 1)
                    nc.scalar.activation(probsT[:, 2 * h:2 * h + 2, :, :].rearrange("p s a n -> p (s a n)"),
                                         ps_probsT[h][:, :], ACT.Copy).then_inc(probsT_copied, 1)

            def attn_high(t):
                act.wait_ge(attn_done, t + 1)
                reached(act, y_done, t)
                nc.scalar.activation(attn_hi[:, :, :, :].rearrange("p j s q -> p s j q"), attn_view, ACT.Copy).then_inc(attn_hi_ready, 1)

            def stage_queries(t):
                reached(act, scores_done, 2 * t)
                nc.scalar.activation(q_tile[:, :, :, :].rearrange("p s j q -> p j s q"),
                                     qkv[:, 0:MEMBERS, cols(t, P)].rearrange("p j (s q) -> p j s q", q=TOKENS),
                                     ACT.Copy).then_inc(q_staged, 1)

            def spread_values(t):
                reached(act, attn_done, t)
                for a in range(2):
                    for g in range(PER_TILE):
                        r, h = divmod(PER_TILE * a + g, 2)
                        nc.scalar.activation(vals_diag[TOKENS * g:TOKENS * (g + 1), :, a, DIM * g:DIM * (g + 1)],
                                             values_t[TOKENS * r:TOKENS * (r + 1), cols(t, PER_TILE),
                                                      DIM * h:DIM * (h + 1)],
                                             ACT.Copy).then_inc(values_spread, 1)

            def gate_exponents(u):
                act.wait_ge(neg_max_ready, u + 1)
                nc.scalar.activation(gate_e[:, :], logit_top[:, 0:2], ACT.Exp, bias=neg_max[:, :],
                                     accum_out=gate_sum[:, :]).then_inc(gate_exp, 1)

            def copy_gatedT(u):
                act.wait_ge(gatedT_done, u + 1)
                reached(act, ffn_done, u)
                nc.scalar.activation(gatedT[:, :], ps_ffn[:, PAIR:PAIR + P], ACT.Copy).then_inc(gatedT_copied, 1)

            def tile_step(t, ahead=2, gate=True):
                copy_probsT(t)
                if ahead >= 1:
                    exponents(t + 1, 0)
                attn_high(t)
                if ahead >= 1:
                    exponents(t + 1, 1)
                if ahead >= 2:
                    stage_queries(t + 2)
                if ahead >= 1:
                    spread_values(t + 1)
                if gate:
                    gate_exponents(t - 2)
                    copy_gatedT(t - 2)

            sum_x(0)
            high_part(0)
            act.wait_ge(in_qkv_rows, 16)
            for n in range(BLOCKS):
                sum_rows(n)
            act.wait_ge(scale_ready, 1)
            scale_qkv(0, 0)
            high_part(1)
            scale_qkv(0, 1)
            sum_x(1)
            scale_qkv(0, 2)
            act.wait_ge(in_wo_rows, 16)
            for n in range(BLOCKS, BLOCKS + PHASES):
                sum_rows(n)
            scale_qkv(1, 0)
            high_part(2)
            sum_x(2)
            sum_x(3)
            scale_qkv(1, 1)
            scale_qkv(1, 2)
            scale_qkv(2, 0)
            high_part(3)
            act.wait_ge(in_woT, 16)
            for j in range(MEMBERS):
                nc.scalar.activation(wo_sign[:, j, :], woT_sb[:, j, :], ACT.Sign).then_inc(act_sign, 1)
            scale_qkv(2, 1)
            act.wait_ge(qkv_guarded, 1)
            stage_queries(0)
            act.wait_ge(values_turned, 1)
            act.wait_ge(pool_const, 3)
            scale_qkv(2, 2)
            spread_values(0)
            scale_qkv(3, 0)
            exponents(0, 0)
            exponents(0, 1)
            scale_qkv(3, 1)
            scale_qkv(3, 2)
            stage_queries(1)
            act.wait_ge(qkv_guarded, PAIRS)
            act.wait_ge(values_turned, PAIRS)
            tile_step(0, gate=False)
            tile_step(1, gate=False)
            with act.Fori(2, TILES - 2) as t:
                tile_step(t)
            tile_step(TILES - 2, ahead=1)
            tile_step(TILES - 1, ahead=0)
            gate_exponents(TILES - 2)
            copy_gatedT(TILES - 2)
            gate_exponents(TILES - 1)
            copy_gatedT(TILES - 1)

        @block.vector
        def _(dve):
            v = nc.vector
            dve.wait_ge(cond_done, 3)
            v.tensor_reduce(mix_top[:, :], bank[2][0:SAMPLES, 0:MIXES], AX_X, ALU.max).then_inc(mix_top_ready, 1)
            dve.wait_ge(mix_top_ready, 1)
            v.tensor_scalar(mix_e[:, :], bank[2][0:SAMPLES, 0:MIXES], mix_top[:, :], None,
                            ALU.subtract).then_inc(mix_shifted, 1)
            dve.wait_ge(mix_exp, 1)
            v.reciprocal(mix_inv[:, :], mix_sum[:, :]).then_inc(mix_inv_ready, 1)
            dve.wait_ge(mix_inv_ready, 1)
            v.scalar_tensor_tensor(out=mix_own[:, :, :],
                                   in0=mix_e[:, :].unsqueeze(1).to_broadcast([SAMPLES, TILES, MIXES]),
                                   scalar=mix_inv[:, :],
                                   in1=cond_sb[0:SAMPLES, COND["own_tile"]].unsqueeze(2)
                                   .to_broadcast([SAMPLES, TILES, MIXES]),
                                   op0=ALU.mult, op1=ALU.mult).then_inc(mix_own_ready, 1)
            dve.wait_ge(att_done, 2)
            v.tensor_copy(attT[:, :], bank[4][0:TILES * MIXES, 0:PER_TILE]).then_inc(attT_ready, 1)
            dve.wait_ge(in_mix_w, 16)
            dve.wait_ge(pool_const, 2)

            def mix_weights(i):
                reached(dve, agg_summed, i)
                tiles = slice(2 * i, 2 * i + 2)
                shares = (att_sb if i else bank[3])[:, 2 * i * MIXES:2 * (i + 1) * MIXES]
                shares = shares.rearrange("p (t k) -> p t k", k=MIXES)
                v.tensor_tensor(prod[:, :, :, :],
                                shares.unsqueeze(2).to_broadcast([P, 2, TOKENS, MIXES]),
                                mix_w_sb[:, :, :].unsqueeze(1).to_broadcast([P, 2, TOKENS, MIXES]),
                                ALU.mult).then_inc(prod_ready, 1)

            def sum_weights(i):
                tiles = slice(2 * i, 2 * i + 2)
                dve.wait_ge(prod_ready, i + 1)
                v.tensor_reduce(agg[:, tiles, :], prod[:, :, :, :], AX_X, ALU.add).then_inc(agg_summed, 1)
                dve.wait_ge(agg_summed, i + 1)
                for q in range(PER_TILE):
                    rows = slice(TOKENS * q, TOKENS * (q + 1))
                    v.tensor_copy(agg_diag[rows, tiles, q, :], agg[rows, tiles, :]).then_inc(agg_ready, 1)

            def full_mixed(i):
                for b in range(2):
                    dve.wait_ge(mixed_done, 2 * i + b + 1)
                    reached(dve, lo_ready, 2 * i)
                    bias = aggb_bc[:, cols(i, PAIR)].unsqueeze(1).to_broadcast([P, 2, PAIR])
                    v.tensor_tensor(mixed[:, 2 * b:2 * b + 2, :],
                                    ps_mixed[b][:, :].rearrange("p (a n) -> p a n", a=2), bias,
                                    ALU.add).then_inc(mixed_full, 1)

            def low_part(i):
                for b in range(2):
                    dve.wait_ge(hi_ready, 2 * i + b + 1)
                    v.tensor_tensor(mixed_lo[:, 2 * b:2 * b + 2, cols(i, PAIR)], mixed[:, 2 * b:2 * b + 2, :],
                                    mixed_hi[:, 2 * b:2 * b + 2, cols(i, PAIR)].bitcast(F32),
                                    ALU.subtract).then_inc(lo_ready, 1)

            def sum_magnitudes(n, values):
                v.tensor_reduce(sums[:, n:n + 1], values, AX_X, ALU.add,
                                apply_absolute_value=True).then_inc(sums_ready, 1)

            def nan_to_num(y, steps, n):
                shape = y.shape[1:]
                low, high, fin = (g[:, 0:int(np.prod(shape))] for g in (g_low, g_high, g_fin))
                if len(shape) == 2:
                    low, high, fin = (g.rearrange("p (a n) -> p a n", a=shape[0]) for g in (low, high, fin))
                v.tensor_scalar(low, y, -NAN_LIMIT, NAN_LIMIT, ALU.max, ALU.min).then_inc(steps[0], 1)
                v.tensor_scalar(high, y, NAN_LIMIT, -NAN_LIMIT, ALU.min, ALU.max).then_inc(steps[1], 1)
                v.tensor_scalar(fin, y, 0.0, 0.0, ALU.mult, ALU.is_equal).then_inc(steps[2], 1)
                dve.wait_ge(steps[0], n)
                dve.wait_ge(steps[1], n)
                v.tensor_tensor(low, low, high, ALU.add).then_inc(steps[3], 1)
                dve.wait_ge(steps[3], n)
                v.tensor_scalar(low, low, 0.5, None, ALU.mult).then_inc(steps[4], 1)
                wait_apart(dve, steps[4], n)
                wait_apart(dve, steps[2], n)
                v.copy_predicated(low, fin, y).then_inc(steps[5], 1)
                dve.wait_ge(steps[5], n)
                return v.tensor_copy(y, low)

            def guard_qkv(i):
                wait_apart(dve, qkv_copied, BLOCKS * (i + 1))
                with dve.If(safe == 1):
                    v.memset(g_low[:, 0:1], 0.0).then_inc(qkv_guarded, 1)
                with dve.Else():
                    for half in range(2):
                        last = nan_to_num(qkv[:, 3 * half:3 * half + 3, cols(i, PAIR)], qkv_guard, 2 * i + half + 1)
                        if half == 0:
                            last.then_inc(qkv_guard[6], 1)
                            dve.wait_ge(qkv_guard[6], i + 1)
                        else:
                            last.then_inc(qkv_guarded, 1)
                dve.wait_ge(qkv_guarded, i + 1)
                v.transpose(values_t[:, 2 * i * PER_TILE:2 * (i + 1) * PER_TILE, :].rearrange("p b d -> p (b d)"),
                            qkv[:, MEMBERS + 1, cols(i, PAIR)]).then_inc(values_turned, 1)

            mix_weights(0)
            sum_weights(0)
            v.tensor_copy(att_sb[:, :], bank[3][:, 0:TILES * MIXES]).then_inc(att_kept, 1)
            dve.wait_ge(aggb_done, 1)
            v.tensor_copy(aggb_bc[:, 0:PAIR], ps_aggb[0][:, 0:PAIR]).then_inc(aggb_ready, 1)
            dve.wait_ge(att_kept, 1)
            dve.wait_ge(aggb_ready, 1)
            full_mixed(0)
            mix_weights(1)
            low_part(0)
            sum_weights(1)
            dve.wait_ge(aggb_done, 2)
            v.tensor_copy(aggb_bc[:, 2 * PAIR:], ps_aggb[1][:, :]).then_inc(aggb_ready, 1)
            v.tensor_copy(aggb_bc[:, PAIR:2 * PAIR], ps_aggb[0][:, PAIR:]).then_inc(aggb_ready, 1)
            mix_weights(2)
            sum_weights(2)
            dve.wait_ge(in_misc, 16)
            dve.wait_ge(row_sums, BLOCKS)
            v.tensor_scalar(scale_in[:, 0:BLOCKS], scale_in[:, 0:BLOCKS], 1.0 / HIDDEN, 1e-8, ALU.mult,
                            ALU.max).then_inc(mean_ready, 1)
            dve.wait_ge(mean_ready, 1)
            v.tensor_tensor(scale_all[:, 0:BLOCKS], scale_in[:, 0:BLOCKS], misc_sb[:, MISC["qkv_scale"]],
                            ALU.mult).then_inc(scale_ready, 1)
            dve.wait_ge(aggb_ready, 3)
            full_mixed(1)
            low_part(1)
            mix_weights(3)
            sum_weights(3)
            full_mixed(2)
            for b in range(2):
                dve.wait_ge(convb_done, b + 1)
                v.tensor_tensor(convb_bc[:, b * HIDDEN:(b + 1) * HIDDEN].rearrange("p (s o) -> p s o", o=TOKENS),
                                ps_convb[b][:, :].rearrange("p (s o) -> p s o", o=TOKENS),
                                cond_sb[:, COND["conv_b"]].unsqueeze(1)
                                .to_broadcast([P, SAMPLES // 2, TOKENS]), ALU.add).then_inc(convb_ready, 1)
            low_part(2)
            dve.wait_ge(row_sums, BLOCKS + PHASES)
            v.tensor_scalar(scale_in[:, BLOCKS:], scale_in[:, BLOCKS:], 1.0 / HIDDEN, 1e-8, ALU.mult,
                            ALU.max).then_inc(mean_ready, 1)
            dve.wait_ge(mean_ready, 2)
            v.tensor_tensor(scale_all[:, BLOCKS:], scale_in[:, BLOCKS:], misc_sb[:, MISC["o_scale"]],
                            ALU.mult).then_inc(scale_ready, 1)
            dve.wait_ge(scale_ready, 2)
            v.tensor_tensor(o_diag[:, :].rearrange("p (a n) -> p a n", a=PHASES),
                            scale_all[:, BLOCKS:].unsqueeze(2).to_broadcast([P, PHASES, P]),
                            ident.unsqueeze(1).to_broadcast([P, PHASES, P]), ALU.mult).then_inc(o_diag_ready, 1)
            dve.wait_ge(agg_summed, PAIRS)
            sum_magnitudes(PAIRS, agg[:, :, :].rearrange("p t o -> p (t o)"))
            sum_magnitudes(PAIRS + 1, aggb_bc[:, :])
            sum_magnitudes(PAIRS + 2, scale_all[:, :])
            full_mixed(3)
            dve.wait_ge(bound_done, 1)
            v.tensor_copy(bound[:, 0:PAIRS + 3], ps_bound[0:1, 0:PAIRS + 3]).then_inc(bound_ready, 1)
            dve.wait_ge(bound_ready, 1)
            by_agg, by_bias, by_scale, x_sum, of_mixed, of_qkv, of_all = (
                bound[:, n:n + 1] for n in range(PAIRS, PAIRS + 7))
            v.tensor_reduce(x_sum, bound[:, 0:PAIRS], AX_X, ALU.add).then_inc(bound_ready, 1)
            dve.wait_ge(bound_ready, 2)
            v.scalar_tensor_tensor(out=of_mixed, in0=x_sum, scalar=by_agg, in1=by_bias,
                                   op0=ALU.mult, op1=ALU.add).then_inc(bound_ready, 1)
            dve.wait_ge(bound_ready, 3)
            v.tensor_scalar(of_qkv, of_mixed, by_scale, float(HIDDEN), ALU.mult, ALU.mult).then_inc(bound_ready, 1)
            dve.wait_ge(bound_ready, 4)
            v.tensor_scalar(of_all, of_qkv, of_qkv, 4.0 * DIM, ALU.mult, ALU.mult).then_inc(bound_ready, 1)
            v.tensor_scalar(of_mixed, of_qkv, by_scale, float(HIDDEN), ALU.mult, ALU.mult).then_inc(bound_ready, 1)
            dve.wait_ge(bound_ready, 6)
            v.tensor_tensor(of_all, of_all, of_mixed, ALU.add).then_inc(bound_ready, 1)
            dve.wait_ge(bound_ready, 7)
            v.tensor_tensor(of_all, of_all, of_qkv, ALU.add).then_inc(bound_ready, 1)
            dve.wait_ge(bound_ready, 8)
            v.tensor_scalar(safe_flag[:, 0:1], of_all, FINITE_BOUND, None, ALU.is_le).then_inc(bound_ready, 1)
            dve.wait_ge(bound_ready, 9)
            safe = dve.value_load(safe_flag[0:1, 0:1], min_val=0, max_val=1)
            dve.wait_ge(o_scale_done, 1)
            v.tensor_copy(o_scale_bc[:, :], ps_o_scale[:, :]).then_inc(o_scale_ready, 1)

            guard_qkv(0)
            low_part(3)
            guard_qkv(1)

            def softmax_shift(t, h):
                scores = ps_scores[h][:, :].rearrange("p (g k) -> p g k", k=TOKENS)
                dve.wait_ge(scores_done, 2 * t + h + 1)
                v.tensor_reduce(row_max[:, h, :], scores, AX_X, ALU.max).then_inc(max_ready, 1)
                dve.wait_ge(max_ready, 2 * t + h + 1)
                reached(dve, probs_ready, 2 * t)
                v.tensor_tensor(probs[:, h, :, :], scores,
                                row_max[:, h, :].unsqueeze(2).to_broadcast([P, HALF, TOKENS]),
                                ALU.subtract).then_inc(shifted, 1)

            def softmax_sum(t, h):
                dve.wait_ge(exp_ready, 2 * t + h + 1)
                v.tensor_reduce(row_sum[:, h, :], probs[:, h, :, :], AX_X, ALU.add).then_inc(sum_ready, 1)
                dve.wait_ge(sum_ready, 2 * t + h + 1)
                v.reciprocal(row_inv[:, h, :], row_sum[:, h, :]).then_inc(inv_ready, 1)

            def attn_low(t):
                dve.wait_ge(attn_hi_ready, t + 1)
                reached(dve, y_done, t)
                v.tensor_tensor(attn_lo[:, :, :, :].rearrange("p j s q -> p s j q"), attn_view,
                                attn_hi[:, :, :, :].rearrange("p j s q -> p s j q").bitcast(F32),
                                ALU.subtract).then_inc(attn_lo_ready, 1)

            def scale_y(t):
                wait_apart(dve, y_done, t + 1)
                reached(dve, x1_ready, t)
                with dve.If(safe == 1):
                    v.tensor_tensor(o_out[:, :], ps_y[:, :], o_scale_bc[:, :], ALU.mult).then_inc(y_scaled, 1)
                with dve.Else():
                    v.tensor_tensor(o_out[:, :], ps_y[:, :], o_scale_bc[:, :], ALU.mult).then_inc(o_guard[6], 1)
                    dve.wait_ge(o_guard[6], t + 1)
                    nan_to_num(o_out[:, :], o_guard, t + 1).then_inc(y_scaled, 1)

            def bias_conv(t):
                dve.wait_ge(conv_done, t + 1)
                reached(dve, ffn_in_done, t)
                bias = convb_bc[:, cols(t, P)].rearrange("p (s o) -> p s o", o=TOKENS)
                v.tensor_tensor(convT[:, :, :, :].rearrange("p a s o -> p s a o"), ps_conv[:, :].rearrange("p (s a o) -> p s a o", s=PER_TILE, a=PHASES),
                                bias.unsqueeze(2).to_broadcast([P, PER_TILE, PHASES, TOKENS]),
                                ALU.add).then_inc(conv_biased, 1)

            def gate_top(u):
                wait_apart(dve, ffn_in_done, u + 1)
                v.max(logit_top[:, :], ps_ffn[:, EXPERTS * RANK:FFN_COLS]).then_inc(top_ready, 1)
                wait_apart(dve, top_ready, u + 1)
                v.max_index(gate_idx[:, :], logit_top[:, :],
                            ps_ffn[:, EXPERTS * RANK:FFN_COLS]).then_inc(gate_idx_ready, 1)
                v.tensor_scalar(neg_max[:, :], logit_top[:, 0:1], -1.0, None, ALU.mult).then_inc(neg_max_ready, 1)

            def gate_masks(u):
                dve.wait_ge(gate_idx_ready, u + 1)
                v.tensor_copy(gate_idx_f[:, :], gate_idx[:, 0:2]).then_inc(idx_f_ready, 1)
                dve.wait_ge(idx_f_ready, u + 1)
                v.tensor_tensor(gate_mask[:, :, :],
                                misc_sb[:, MISC["iota"]].unsqueeze(1).to_broadcast([P, 2, EXPERTS]),
                                gate_idx_f[:, :].unsqueeze(2).to_broadcast([P, 2, EXPERTS]),
                                ALU.is_equal).then_inc(gate_mask_ready, 1)

            def gate_weights(u):
                dve.wait_ge(gate_exp, u + 1)
                v.reciprocal(gate_inv[:, :], gate_sum[:, :]).then_inc(gate_inv_ready, 1)
                dve.wait_ge(gate_mask_ready, u + 1)
                v.scalar_tensor_tensor(out=gate_w[:, :], in0=gate_mask[:, 1, :], scalar=gate_e[:, 1:2],
                                       in1=gate_mask[:, 0, :], op0=ALU.mult, op1=ALU.add).then_inc(gate_w_ready, 1)

            def gate_apply(u):
                dve.wait_ge(gate_w_ready, u + 1)
                dve.wait_ge(gate_inv_ready, u + 1)
                reached(dve, gatedT_done, u)
                v.scalar_tensor_tensor(out=gated[:, :].rearrange("p (e r) -> p e r", r=RANK),
                                       in0=ps_ffn[:, 0:EXPERTS * RANK].rearrange("p (e r) -> p e r", r=RANK),
                                       scalar=gate_inv[:, :],
                                       in1=gate_w[:, :].unsqueeze(2).to_broadcast([P, EXPERTS, RANK]),
                                       op0=ALU.mult, op1=ALU.mult).then_inc(gated_ready, 1)

            def finish(u):
                dve.wait_ge(ffn_done, u + 1)
                dve.wait_ge(x1_ready, u + 1)
                if isinstance(u, int):
                    dst, res = x1[:, u, :], x1[:, u, :]
                else:
                    dst = x1[:, bass.ds(u, 1), :].rearrange("p a n -> p (a n)")
                    res = x1[:, bass.ds(u, 1), :].rearrange("p a n -> p (a n)")
                v.scalar_tensor_tensor(out=dst, in0=ps_y[:, :], scalar=8.0 / RANK, in1=res, op0=ALU.mult,
                                       op1=ALU.add).then_inc(out_ready, 1)

            def tile_step(t, scores=True, up=True, down=True):
                if up:
                    bias_conv(t - 2)
                if down:
                    finish(t - 3)
                if scores:
                    softmax_shift(t + 1, 0)
                    softmax_shift(t + 1, 1)
                attn_low(t)
                if scores:
                    softmax_sum(t + 1, 0)
                if up:
                    gate_top(t - 2)
                if scores:
                    softmax_sum(t + 1, 1)
                if up:
                    gate_masks(t - 2)
                    gate_weights(t - 2)
                scale_y(t)
                if up:
                    gate_apply(t - 2)

            softmax_shift(0, 0)
            softmax_shift(0, 1)
            guard_qkv(2)
            softmax_sum(0, 0)
            softmax_sum(0, 1)
            guard_qkv(3)
            dve.wait_ge(o_scale_ready, 1)
            dve.wait_ge(convb_ready, 2)
            tile_step(0, up=False, down=False)
            tile_step(1, up=False, down=False)
            tile_step(2, down=False)
            with dve.Fori(3, TILES - 1) as t:
                tile_step(t)
            tile_step(TILES - 1, scores=False)
            bias_conv(TILES - 2)
            finish(TILES - 3)
            for u in (TILES - 2, TILES - 1):
                if u == TILES - 1:
                    bias_conv(u)
                gate_top(u)
                gate_masks(u)
                gate_weights(u)
                gate_apply(u)
                finish(u)

        @block.tensor
        def _(pe):
            mm = nc.tensor.matmul
            pe.wait_ge(in_cond, 16)
            mm(bank[0][:, 0:SAMPLES], cond_sb[:, COND["W0"]], cond_sb[:, COND["condT"]], start=True,
               stop=True).then_inc(cond_done, 1)
            pe.wait_ge(cond_gelu, 1)
            mm(bank[1][:, 0:SAMPLES], cond_sb[:, COND["W1"]], gelu0[:, :], start=True, stop=True).then_inc(cond_done, 1)
            pe.wait_ge(cond_gelu, 2)
            pe.wait_ge(pool_const, 1)
            mm(bank[2][0:SAMPLES, 0:MIXES], gelu1[:, :], cond_sb[:, COND["W2"]], start=True, stop=False)
            mm(bank[2][0:SAMPLES, 0:MIXES], ones[0:1, 0:SAMPLES], cond_sb[0:1, COND["b2"]], start=False,
               stop=True).then_inc(cond_done, 1)

            def sum_conv_bias(b):
                half = slice(b * SAMPLES // 2, (b + 1) * SAMPLES // 2)
                mm(ps_convb[b][:, :], ones[:, :], outer[:, half, :].rearrange("p b o -> p (b o)"),
                   start=True, stop=True).then_inc(convb_done, 1)

            pe.wait_ge(outer_done, 1)
            sum_conv_bias(0)
            spread = cond_sb[0:SAMPLES, COND["spread"]]
            own = mix_own[:, :, :].rearrange("p t k -> p (t k)")
            pe.wait_ge(mix_own_ready, 1)
            mm(bank[4][0:TILES * MIXES, 0:PER_TILE], own, spread[:, 0:P:TOKENS], start=True, stop=True).then_inc(att_done, 1)
            mm(bank[3][:, 0:TILES * MIXES], spread, own, start=True, stop=True).then_inc(att_done, 1)
            sum_conv_bias(1)

            def sum_mix_bias(dst, tiles):
                return mm(dst, ones[0:TILES * MIXES, :], outer_b[:, tiles, :, :].rearrange("p t q o -> p (t q o)"),
                          start=True, stop=True)

            def mix(i):
                pe.wait_ge(in_pair[i], 16)
                pe.wait_ge(agg_ready, PER_TILE * (i + 1))
                reached(pe, mixed_full, 2 * i)
                for b in range(2):
                    for ph in (2 * b, 2 * b + 1):
                        for a in range(2):
                            at = (ph % 2) * PAIR + a * P
                            last = mm(ps_mixed[b][:, at:at + P],
                                      x_all[:, 2 * i + a, ph * STEPS:(ph + 1) * STEPS],
                                      agg_diag[:, 2 * i + a, :, :].rearrange("p q o -> p (q o)"),
                                      start=True, stop=True)
                    last.then_inc(mixed_done, 1)

            def project(i, b):
                reached(pe, qkv_copied, BLOCKS * (i - 1) + 2 * (b + 1) if i else 0)
                for n in (2 * b, 2 * b + 1):
                    dst = ps_qkv[b][:, (n % 2) * PAIR:(n % 2 + 1) * PAIR]
                    for ph in range(PHASES):
                        w = qkv_sign[:, ph, n * P:(n + 1) * P]
                        mm(dst, w, mixed_hi[:, ph, cols(i, PAIR)], start=(ph == 0), stop=False)
                        last = mm(dst, w, mixed_lo[:, ph, cols(i, PAIR)], start=False, stop=(ph == PHASES - 1))
                last.then_inc(qkv_done, 1)

            def bound_and_scales():
                pe.wait_ge(convb_ready, 2)
                pe.wait_ge(sums_ready, 3)
                pe.wait_ge(x_sums, PAIRS)
                mm(ps_bound[0:1, 0:PAIRS + 3], ones[:, 0:1], sums[:, :], start=True, stop=True).then_inc(bound_done, 1)
                mm(ps_o_scale[:, :], ones[:, :], o_diag[:, :], start=True, stop=True).then_inc(o_scale_done, 1)

            def pair_step(i):
                pe.wait_ge(hi_ready, 2 * (i + 1))
                pe.wait_ge(lo_ready, 2 * (i + 1))
                project(i, 0)
                if i < PAIRS - 1:
                    mix(i + 1)
                if i == 2:
                    bound_and_scales()
                if i == 0:
                    pe.wait_ge(att_kept, 1)
                project(i, 1)
                if i == 0:
                    pe.wait_ge(aggb_ready, 3)
                project(i, 2)

            pe.wait_ge(outer_b_ready, 1)
            sum_mix_bias(ps_aggb[0][:, 0:PAIR], slice(0, 2)).then_inc(aggb_done, 1)
            mix(0)
            pe.wait_ge(outer_b_ready, 2)
            pe.wait_ge(aggb_ready, 1)
            sum_mix_bias(ps_aggb[0][:, PAIR:], slice(2, 4))
            sum_mix_bias(ps_aggb[1][:, :], slice(4, TILES)).then_inc(aggb_done, 1)
            pe.wait_ge(act_sign, PHASES)
            pair_step(0)
            pair_step(1)
            pair_step(2)

            def score(t):
                pe.wait_ge(q_staged, t + 1)
                pe.wait_ge(keys_spread, t + 1)
                reached(pe, shifted, 2 * t)
                for s in range(PER_TILE):
                    last = mm(ps_scores[s // 2][:, (s % 2) * PAIR:(s % 2 + 1) * PAIR],
                              q_tile[:, s, :, :],
                              keys_diag[:, s, :, :].rearrange("p g k -> p (g k)"), start=True, stop=True)
                    if s % 2:
                        last.then_inc(scores_done, 1)

            def turn_probs(t):
                for h in range(2):
                    pe.wait_ge(probs_ready, 2 * t + h + 1)
                    reached(pe, probsT_copied, 2 * t)
                    for s in (2 * h, 2 * h + 1):
                        for a in range(2):
                            at = ((s % 2) * 2 + a) * P
                            last = nc.tensor.transpose(ps_probsT[h][:, at:at + P], probs_n[:, s, PER_TILE * a:PER_TILE * (a + 1), :], ident)
                    last.then_inc(probsT_done, 1)

            def attend(t):
                pe.wait_ge(values_spread, GROUPS * (t + 1))
                reached(pe, attn_lo_ready, t)
                for s in range(PER_TILE):
                    pe.wait_ge(probsT_copied, 2 * t + s // 2 + 1)
                    for a in range(2):
                        last = mm(ps_attn[a * P // 2:(a + 1) * P // 2, s * P:(s + 1) * P], vals_diag[:, s, a, :],
                                  probsT[:, s, a, :], start=True, stop=True)
                last.then_inc(attn_done, 1)

            def project_out(t):
                pe.wait_ge(attn_hi_ready, t + 1)
                pe.wait_ge(attn_lo_ready, t + 1)
                reached(pe, y_scaled, t)
                reached(pe, out_ready, t - 2)
                for j in range(MEMBERS):
                    for part in (attn_hi, attn_lo):
                        last = mm(ps_y[:, :], part[:, j, :, :], wo_sign[:, j, :],
                                  start=(j == 0 and part is attn_hi), stop=(j == MEMBERS - 1 and part is attn_lo))
                last.then_inc(y_done, 1)

            def convolve(t):
                pe.wait_ge(phased, 16 * PHASES * (t + 1))
                reached(pe, conv_biased, t)
                for s in range(PER_TILE):
                    for shift in range(3):
                        last = mm(ps_conv[:, s * P:(s + 1) * P], x1_phased[:, s, shift:shift + STEPS],
                                  conv_w_sb[:, shift, :], start=(shift == 0), stop=(shift == 2))
                last.then_inc(conv_done, 1)

            def ffn_up(t):
                pe.wait_ge(conv_biased, t + 1)
                for ph in range(PHASES):
                    mm(ps_ffn[:, 0:FFN_COLS], convT[:, ph, :, :], ffn_in_sb[:, ph, :],
                              start=(ph == 0), stop=False)
                last = mm(ps_ffn[:, EXPERTS * RANK:FFN_COLS], ones[0:1, :], misc_sb[0:1, MISC["router_b"]],
                          start=False, stop=True)
                last.then_inc(ffn_in_done, 1)

            def turn_gated(u):
                pe.wait_ge(gated_ready, u + 1)
                reached(pe, gatedT_copied, u)
                nc.tensor.transpose(ps_ffn[:, PAIR:PAIR + P], gated[:, :], ident).then_inc(gatedT_done, 1)

            def ffn_down(u):
                pe.wait_ge(gatedT_copied, u + 1)
                pe.wait_ge(y_scaled, u + 3 if not isinstance(u, int) else min(u + 3, TILES))
                reached(pe, out_ready, u)
                mm(ps_y[:, :], gatedT[:, :], ffn_out_sb[:, :], start=True, stop=True).then_inc(ffn_done, 1)

            def tile_step(t, scores=True, conv=True, up=True, down=True):
                turn_probs(t)
                if down:
                    ffn_down(t - 3)
                if scores:
                    score(t + 1)
                attend(t)
                if up:
                    ffn_up(t - 2)
                project_out(t)
                if conv:
                    convolve(t - 1)
                if up:
                    turn_gated(t - 2)

            pe.wait_ge(bound_ready, 1)
            pe.wait_ge(o_scale_ready, 1)
            score(0)
            pair_step(3)
            pe.wait_ge(pool_const, 4)
            pe.wait_ge(in_misc, 16)
            pe.wait_ge(in_ffn, 32)
            pe.wait_ge(in_conv, 16)
            pe.wait_ge(act_sign, PHASES + MEMBERS)
            pe.wait_ge(mixed_full, 2 * PAIRS)
            pe.wait_ge(qkv_copied, BLOCKS * PAIRS)
            score(1)
            tile_step(0, scores=False, conv=False, up=False, down=False)
            tile_step(1, up=False, down=False)
            tile_step(2, down=False)
            with pe.Fori(3, TILES - 1) as t:
                tile_step(t)
            tile_step(TILES - 1, scores=False)
            ffn_down(TILES - 3)
            ffn_up(TILES - 2)
            turn_gated(TILES - 2)
            ffn_down(TILES - 2)
            convolve(TILES - 1)
            ffn_up(TILES - 1)
            turn_gated(TILES - 1)
            ffn_down(TILES - 1)


def kernel(**inputs):
    import numpy as np
    import concourse.bacc as bacc
    from concourse.bass_utils import run_bass_kernel_spmd

    f = {k: np.asarray(a) for k, a in inputs.items()}
    dt = f["x"].dtype

    def phased(a):
        return np.ascontiguousarray(a.reshape(*a.shape[:-1], STEPS, PHASES).swapaxes(-1, -2)).reshape(a.shape)

    def head_order(a):
        return a.reshape(GROUPS, MEMBERS, DIM, *a.shape[1:]).swapaxes(0, 1).reshape(a.shape)

    def pack(widths, parts):
        cols_of, total = columns(widths)
        out = np.zeros((P, total), dt)
        for name, a in parts.items():
            out[:, cols_of[name]] = a
        return out

    rows = np.arange(P)
    cond_pack = pack(COND_COLS, dict(
        condT=f["cond_128"].T, W0=f["L0_cond_W0"], b0=f["L0_cond_b0"][:, None], W1=f["L0_cond_W1"],
        b1=f["L0_cond_b1"][:, None], W2=f["L0_cond_W2"], b2=f["L0_cond_b2"][None, :],
        cwT=f["L0_cond2_c_weight"].T, conv_b=f["fside_S_0"][None, :],
        spread=(rows[:, None] % PER_TILE == rows[None, :] // TOKENS),
        own_tile=(rows[:, None] // PER_TILE == np.arange(TILES)[None, :])))
    qkv_scale = np.concatenate([head_order(f["L0_attn_q_scale"]), f["L0_attn_k_scale"], f["L0_attn_v_scale"]])
    misc = pack(MISC_COLS, dict(
        ident=np.eye(P, dtype=dt), headmask=(rows[:, None] // DIM == np.arange(GROUPS)[None, :]),
        iota=np.arange(EXPERTS)[None, :], router_b=f["L0_ffn_router_b"][None, :],
        qkv_scale=qkv_scale.reshape(BLOCKS, P).T, o_scale=phased(f["L0_attn_o_scale"]).reshape(PHASES, P).T))
    mix_w = np.tile(f["L0_cond_weight"][..., 0].transpose(2, 1, 0), (PER_TILE, 1, 1))
    mix_b = np.zeros((TILES, MIXES, TILES, TOKENS), dt)
    for t in range(TILES):
        mix_b[t, :, t, :] = f["L0_cond_bias_k"]
    w_rows = np.concatenate([head_order(f["L0_attn_q_weight"]), f["L0_attn_k_weight"], f["L0_attn_v_weight"]])
    w_rows = phased(w_rows)
    qkvT = np.ascontiguousarray(w_rows.T).reshape(PHASES, P, BLOCKS * P)
    qkv_rows = w_rows.reshape(BLOCKS, P, HIDDEN).transpose(1, 0, 2)
    wo = phased(f["L0_attn_o_weight"].T)
    woT = head_order(wo).reshape(MEMBERS, P, HIDDEN).transpose(1, 0, 2)
    wo_rows = wo.T.reshape(PHASES, P, HIDDEN).transpose(1, 0, 2)
    w = f["L0_cond2_weight"]
    per_group = w.shape[1]
    conv_w = np.zeros((PHASES, TOKENS, 3, PHASES, TOKENS), dt)
    for shift in range(3):
        for src in range(PHASES):
            for dst in range(PHASES):
                tap = PHASES * (shift - 1) + src - dst + w.shape[2] // 2
                if 0 <= tap < w.shape[2]:
                    for o in range(TOKENS):
                        first = o // per_group * per_group
                        conv_w[src, first:first + per_group, shift, dst, o] = w[o, :, tap]
    ffn_in = np.concatenate([f["L0_ffn_A"].reshape(EXPERTS * RANK, HIDDEN), f["L0_ffn_router_w"]])
    ffn_in = phased(ffn_in).T.reshape(PHASES, P, FFN_COLS).transpose(1, 0, 2)
    ffn_out = phased(f["L0_ffn_Bm"].transpose(0, 2, 1).reshape(EXPERTS * RANK, HIDDEN))

    arrays = dict(
        cond_pack=cond_pack, misc=misc, mix_w=mix_w, mix_b=mix_b.reshape(TILES * MIXES, TILES, TOKENS),
        x_rows=phased(f["x"]).reshape(ROWS, HIDDEN), qkvT=qkvT, qkv_rows=qkv_rows, woT=woT, wo_rows=wo_rows,
        conv_w=conv_w.reshape(P, 3, P), ffn_in=ffn_in, ffn_out=ffn_out)
    arrays = {k: np.ascontiguousarray(a) for k, a in arrays.items()}
    nc = bacc.Bacc("TRN2", target_bir_lowering=False, num_devices=1)
    args = {k: nc.dram_tensor(f"in_{k}", a.shape, mybir.dt.from_np(a.dtype), kind="ExternalInput").ap()
            for k, a in arrays.items()}
    out = nc.dram_tensor("out_rows", (ROWS, HIDDEN), F32, kind="ExternalOutput").ap()
    build(nc, out=out, **args)
    r = run_bass_kernel_spmd(nc, [{f"in_{k}": a for k, a in arrays.items()}], core_ids=[0])
    got = r.results[0]["out_rows"]
    return got.reshape(SAMPLES, TOKENS, PHASES, STEPS).swapaxes(-1, -2).reshape(SAMPLES, TOKENS, HIDDEN)
```
